# Optimizing a Trainium2 kernel written in Bass

```python
import numpy as np
import jax
import jax.numpy as jnp

def _softmax(x, axis=-1):
    return jax.nn.softmax(x, axis=axis)

def _gelu(x):
    return jax.nn.gelu(x, approximate=True)

def _silu(x):
    return jax.nn.silu(x)

def _sigmoid(x):
    return jax.nn.sigmoid(x)

def _layernorm(x, axis=-1, eps=1e-05):
    m = jnp.mean(x, axis=axis, keepdims=True)
    v = jnp.var(x, axis=axis, keepdims=True)
    return (x - m) / jnp.sqrt(v + eps)

def _scatter_add(tgt, idx, src, axis=0):
    return tgt.at[idx].add(src)

def _segment_sum(src, seg, n):
    return jax.ops.segment_sum(src, seg, n)
kernel_name = 'mk_adj_resnorm_d2_adj_r2_3bf313'

def setup_inputs(seed: int=0):
    np.random.seed(seed)
    _w = jnp.asarray

    def _rec_inputs():
        import jax
        import jax.numpy as jnp
        _gk = jax.random.key(seed)
        x = -0.0005207 + 1.001 * jax.random.normal(jax.random.fold_in(_gk, 1), (4096, 128), jnp.float32)
        _w = (1.0 + jnp.arange(4096, dtype=jnp.float32)) ** (-0.5)
        _w = _w / _w.mean()
        _pij = jnp.clip(0.00390625 * _w[:, None] * _w[None, :], 0.0, 1.0)
        _a = jax.random.uniform(jax.random.fold_in(_gk, 2), (4096, 4096)) < _pij
        _af = _a.astype(jnp.float32)
        adj = _af
        return (x, adj)
    x, adj = _rec_inputs()

    def _L0_gnn_setup():
        import jax, jax.numpy as jnp
        import numpy as np
        N = 4096
        DIN = 128
        DOUT = 128
        EDGE_P = 0.004
        key = jax.random.key(seed)
        k1, k2, k3, k4, k5 = jax.random.split(key, 5)
        h = jax.random.normal(k1, (N, DIN), dtype=jnp.float32)
        adj = (jax.random.uniform(k2, (N, N)) < EDGE_P).astype(jnp.float32)
        xav_w = float(np.sqrt(6.0 / (DIN + DOUT)))
        weight = jax.random.uniform(k3, (DIN, DOUT), minval=-xav_w, maxval=xav_w, dtype=jnp.float32)
        xav_a = float(np.sqrt(6.0 / (DOUT + 1)))
        a_l = jax.random.uniform(k4, (DOUT,), minval=-xav_a, maxval=xav_a, dtype=jnp.float32)
        a_r = jax.random.uniform(k5, (DOUT,), minval=-xav_a, maxval=xav_a, dtype=jnp.float32)
        b = jnp.zeros((DOUT,), dtype=jnp.float32)
        return {'h': h, 'adj': adj, 'weight': weight, 'a_l': a_l, 'a_r': a_r, 'b': b}
    _L0_gnn_all = _L0_gnn_setup()
    _L0_gnn_in = {k: v for k, v in _L0_gnn_all.items() if k in ('weight', 'a_l', 'a_r', 'b')}
    del _L0_gnn_all

    def _L1_gnn_setup():
        import jax, jax.numpy as jnp
        import numpy as np
        N = 4096
        IN_F = 128
        OUT_F = 128
        ATTN_DIM = 2
        NEG_INF = -1e+18
        key = jax.random.key(seed)
        k1, k2, k3, k4, k5 = jax.random.split(key, 5)
        node_feats = jax.random.normal(k1, (N, IN_F), dtype=jnp.float32)
        Ahat = (jax.random.uniform(k2, (N, N)) < 0.01).astype(jnp.float32)
        Ahat = Ahat.at[jnp.arange(N), jnp.arange(N)].set(1.0)
        bound_w = 1.0 / np.sqrt(IN_F)
        bound_wa = 1.0 / np.sqrt(OUT_F)
        bound_a = 1.0 / np.sqrt(2 * ATTN_DIM)
        w = jax.random.uniform(k3, (IN_F, OUT_F), minval=-bound_w, maxval=bound_w, dtype=jnp.float32)
        w_a = jax.random.uniform(k4, (OUT_F, ATTN_DIM), minval=-bound_wa, maxval=bound_wa, dtype=jnp.float32)
        a = jax.random.uniform(k5, (2 * ATTN_DIM, 1), minval=-bound_a, maxval=bound_a, dtype=jnp.float32)
        return {'node_feats': node_feats, 'Ahat': Ahat, 'w': w, 'w_a': w_a, 'a': a}
    _L1_gnn_all = _L1_gnn_setup()
    _L1_gnn_in = {k: v for k, v in _L1_gnn_all.items() if k in ('w', 'w_a', 'a')}
    del _L1_gnn_all
    return {'x': x, 'adj': adj, 'L0_gnn_weight': _L0_gnn_in['weight'], 'L0_gnn_a_l': _L0_gnn_in['a_l'], 'L0_gnn_a_r': _L0_gnn_in['a_r'], 'L0_gnn_b': _L0_gnn_in['b'], 'L1_gnn_w': _L1_gnn_in['w'], 'L1_gnn_w_a': _L1_gnn_in['w_a'], 'L1_gnn_a': _L1_gnn_in['a']}

def reference(x, adj, L0_gnn_weight, L0_gnn_a_l, L0_gnn_a_r, L0_gnn_b, L1_gnn_w, L1_gnn_w_a, L1_gnn_a):
    import jax
    import jax.numpy as jnp

    def _L0_gnn_ref(h, adj, weight, a_l, a_r, b):
        import jax, jax.numpy as jnp
        import numpy as np
        N = 4096
        DIN = 128
        DOUT = 128
        EDGE_P = 0.004
        x = h @ weight
        el = x @ a_l
        er = x @ a_r
        mask = adj != 0
        scores = el[:, None] + er[None, :]
        attn = jnp.exp(jax.nn.leaky_relu(scores, negative_slope=0.2))
        attn = jnp.where(mask, attn, 0.0)
        denom = jnp.maximum(attn.sum(axis=-1, keepdims=True), 1e-12)
        A = attn / denom
        out = A @ x + b
        return out

    def _L1_gnn_ref(node_feats, Ahat, w, w_a, a):
        import jax, jax.numpy as jnp
        import numpy as np
        N = 4096
        IN_F = 128
        OUT_F = 128
        ATTN_DIM = 2
        NEG_INF = -1e+18
        h_prime = node_feats @ w
        h_reduced = h_prime @ w_a
        f_src = (h_reduced @ a[:ATTN_DIM]).squeeze(-1)
        f_dst = (h_reduced @ a[ATTN_DIM:]).squeeze(-1)
        e = f_src[:, None] + f_dst[None, :]
        masked_e = jnp.where(Ahat > 0, e, NEG_INF)
        attn_scores = jax.nn.softmax(masked_e, axis=-1)
        out = attn_scores @ h_prime
        return jax.nn.relu(out)
    x = _layernorm(x + _L0_gnn_ref(x, adj, L0_gnn_weight, L0_gnn_a_l, L0_gnn_a_r, L0_gnn_b), axis=-1)
    x = _layernorm(x + _L1_gnn_ref(x, adj, L1_gnn_w, L1_gnn_w_a, L1_gnn_a), axis=-1)
    return x

_drawn_inputs = setup_inputs


def setup_inputs(seed=0):
    import zlib

    import numpy as np

    out = dict(_drawn_inputs(seed))
    spreads = {'L0_gnn_b': (0.0, 0.1)}
    factors = {'L1_gnn_w_a': 4.115, 'L1_gnn_a': 8.0}
    for name, (base, spread) in spreads.items():
        noise = np.random.default_rng([zlib.crc32(name.encode()), seed]).standard_normal(out[name].shape)
        drawn = base * np.exp(spread * noise) if base else spread * noise
        out[name] = jnp.asarray(drawn.astype(out[name].dtype))
    for name, factor in factors.items():
        out[name] = (out[name] * factor).astype(out[name].dtype)
    return out
```

```python
from contextlib import ExitStack

import numpy as np

import concourse.bass as bass
from concourse import mybir

ALU = mybir.AluOpType
ACT = mybir.ActivationFunctionType
F32 = mybir.dt.float32
F16 = mybir.dt.float16
BF16 = mybir.dt.bfloat16
I8 = mybir.dt.int8
I32 = mybir.dt.int32
AX = mybir.AxisListType

P = 128
N = 4096
D = 128
DA = D + 1
DV = D + 2
TILES = N // P
HALF = N // 2
HB = HALF // P
QB = HB // 2
RING = 4
AHEAD = 2
BANK = 512
PER_BANK = BANK // DA
BANKS = -(-HB // PER_BANK)
SLOTS = BANKS * PER_BANK
GROUP = 4
GROUPS = TILES // GROUP
FIN = 4
A_GROUPS = GROUPS // 2
RESIDENT = TILES // 2
SWEEPS0 = 2
L1 = 2
SLOPE = 0.2
EPS = 1e-5
TINY = 1e-12
LOG2E = 1.4426950408889634
LN2_HI = 355.0 / 512.0
LN2_LO = -2.12194440e-4
EXPONENT = 1 << 23
EXP_MASK = 0x7F800000
V_SCALE = 13
W_WIDTHS = [D + 2, D, D, D, D, P, 2, P, 1]
W_AT = [sum(W_WIDTHS[:k]) for k in range(len(W_WIDTHS) + 1)]
W_COLS = W_AT[-1]
NEG_INF = -1e18
TE_LOW, TE_HIGH = 47.0, 187.0


class Chain:

    def __init__(self, eng, sem, call, per):
        self.eng, self.sem, self.call, self.per, self.k = eng, sem, call, per, 0

    def inc(self, ins):
        self.k += 1
        ins.then_inc(self.sem, 1)

    def wait(self):
        self.eng.wait_ge(self.sem, self.call * self.per + self.k)

    def step(self, ins):
        self.inc(ins)
        self.wait()

    def end(self):
        assert self.k == self.per, (self.k, self.per)


class Tile:

    def __init__(self, w, base, i=0):
        self.w, self.base, self.i = w, base, i
        self.jt = base + i * RING
        self.n = w * TILES + self.jt
        self.slot = base % RING
        self.resident = base % 2 == 0
        self.half = base // 2 + i * (RING // 2)
        self.again_slot = base // 2 % 2
        self.n_after_ring = w > 0 or base >= RING
        self.first = isinstance(i, int) and base == 0
        self.last = isinstance(i, int) and base == TILES - 1

    def ahead(self, k):
        if self.base + k >= TILES and isinstance(self.i, int):
            return Tile(self.w + 1, self.base + k - TILES)
        return Tile(self.w, self.base + k, self.i)


def turns(eng, w, lo, n, tile, before=None):
    with eng.Fori(0, n) as i:
        if before:
            before(i)
        for u in range(RING):
            tile(Tile(w, lo + u, i))


def build(nc, adjT, adj, xT, x, weights_d, out):
    with ExitStack() as ctx:
        def sb(name, shape, dt=F32):
            return ctx.enter_context(nc.sbuf_tensor(name, shape, dt))

        def sem(name):
            return ctx.enter_context(nc.semaphore(name))

        signs = sb("signs", [P, RESIDENT, N], I8)
        adj_ring = sb("adj_ring", [P, RING, HALF])
        pair = sb("pair", [P, RING, HALF])
        pair16 = pair[:, :, :].bitcast(BF16)
        V = sb("V", [P, TILES * 2 * DV], F16)
        V_v = V[:, :].rearrange("p (t c) -> p t c", c=2 * DV)
        elb = [V[:, h * HB * 2 * DV:h * HB * 2 * DV + 2 * HALF].bitcast(F32) for h in range(2)]
        haug = sb("haug", [P, TILES, DA])
        obuf = haug[:, 0:HB, 0:D]
        fin = haug[:, HB:2 * HB, 0:D]
        xs = sb("xs", [P, TILES, D])
        read0 = sb("read0", [P, HB - BANKS // 2 * PER_BANK, D])
        xT_sb = signs[:, RESIDENT - 4:RESIDENT, :].rearrange("p t n -> p (t n)").bitcast(F32)
        weights = sb("weights", [P, W_COLS])
        w0, w0T, w1_sb, w1T_sb, bb, ident, alr, waT_f, adst_f = (
            weights[:, a:z] for a, z in zip(W_AT, W_AT[1:]))
        waT, adst = waT_f[0:2, :], adst_f[0:2, :]
        wad = sb("wad", [P, 1])
        wf = sb("wf", [P, 1])
        ones = sb("ones", [P, D])
        walb = sb("walb", [P, P])
        xmb = sb("xmb", [P, P])
        zeros = sb("zeros", [P, PER_BANK * DA], BF16)
        elr = sb("elr", [P, TILES, 2])
        Fj = sb("Fj", [P, TILES])
        fe = sb("fe", [P, 2, SLOTS])
        den = sb("den", [P, SLOTS])
        coef = sb("coef", [P, SLOTS])
        none = sb("none", [P, SLOTS])
        stats = sb("stats", [P, GROUP, 6])
        scratch = sb("scratch", [P, 2])
        mv = [sb(f"mv{k}", [P, GROUP, 2]) for k in range(2)]
        veps = [sb(f"veps{k}", [P, GROUP]) for k in range(2)]
        rstd = [sb(f"rstd{k}", [P, GROUP]) for k in range(2)]
        half_neg = sb("half_neg", [P, GROUP])
        x1n = sb("x1n", [P, GROUP, D])
        x1T = sb("x1T", [P, GROUP * P])
        xsum = sb("xsum", [P, GROUPS])
        xtot = sb("xtot", [P, 1])
        hmean = sb("hmean", [P, D])
        k_int = sb("k_int", [P, GROUP], I32)
        u1 = sb("u1", [P, GROUP])
        u2 = sb("u2", [P, GROUP])
        rj = sb("rj", [P, GROUP])
        hmax = sb("hmax", [P, GROUP])
        hmax1 = sb("hmax1", [P, GROUP])
        hexp = sb("hexp", [P, GROUP], I32)
        hinv = sb("hinv", [P, GROUP], I32)
        q = sb("q", [P, GROUP])
        kf = sb("kf", [P, TILES])
        hef = sb("hef", [P, TILES])
        te = sb("te", [P, TILES])
        tec = sb("tec", [P, TILES])
        pj = sb("pj", [P, TILES], I32)
        pj_f = pj[:, :].bitcast(F32)
        kpart = sb("kpart", [P, 1])
        k1 = sb("k1", [1, 1])
        Kb = sb("Kb", [P, 1])
        far = sb("far", [P, 2, TILES])
        far_any = sb("far_any", [P, 1])
        flag = sb("flag", [1, 1], I32)
        fb = V[:, 0:2 * N].bitcast(F32)
        hfull = haug[:, :, 0:D]
        adj_row = adj_ring[:, 0:2, :].rearrange("p a n -> p (a n)")
        e_row = pair[:, 0:2, :].rearrange("p a n -> p (a n)")
        t_row = pair[:, 2:4, :].rearrange("p a n -> p (a n)")
        wfb = sb("wfb", [P, P])
        g_max = sb("g_max", [P, 1])
        g_sum = sb("g_sum", [P, 1])
        g_rec = sb("g_rec", [P, 1])
        g_y = sb("g_y", [P, D])
        g_out = sb("g_out", [P, D])

        acc = ctx.enter_context(nc.psum_tensor("acc", [P, BANKS, BANK], F32))
        ps_t = ctx.enter_context(nc.psum_tensor("ps_t", [P, BANK], F32))
        ps_h = ctx.enter_context(nc.psum_tensor("ps_h", [P, BANK], F32))
        small = [ps_t, ps_h]

        def el_bank(c):
            return acc[:, c, :] if c < 4 else small[c % 2][:, :]

        def acc_of(block, bank0=0):
            c = block % PER_BANK * DA
            return acc[:, bank0 + block // PER_BANK, c:c + DA]

        def den_of(bank0, banks):
            return acc[:, bank0:bank0 + banks, 0:PER_BANK * DA].rearrange(
                "p k (s c) -> p k s c", c=DA)[:, :, :, D]

        def by_bank(t, banks):
            return t[:, 0:banks * PER_BANK].rearrange("p (k s) -> p k s", s=PER_BANK)

        w_in = sem("w_in")
        xT_in = [sem(f"xT_in{c}") for c in range(4)]
        x_in = sem("x_in")
        consts = sem("consts")
        wa_done = sem("wa_done")
        wa_copied = sem("wa_copied")
        el_done = sem("el_done")
        el_copied = sem("el_copied")
        h0_done = sem("h0_done")
        elr_copied = sem("elr_copied")
        F_done = sem("F_done")
        haug_done = sem("haug_done")
        fe_done = sem("fe_done")
        xb_done = sem("xb_done")
        adj_in = [sem(f"adj_in{s}") for s in range(RING)]
        again_in = [sem(f"again_in{s}") for s in range(2)]
        scored_v = sem("scored_v")
        scored_a = sem("scored_a")
        exped = sem("exped")
        masked = sem("masked")
        scaled_v = sem("scaled_v")
        scaled_a = sem("scaled_a")
        tile_used = sem("tile_used")
        coef_done = sem("coef_done")
        freed_v = sem("freed_v")
        freed_a = sem("freed_a")
        y0_added = sem("y0_added")
        own = {k: sem(f"own_{k}") for k in ("y", "var", "pow", "parts", "mask", "coef", "last", "k", "far")}
        var_done = sem("var_done")
        rstd_done = sem("rstd_done")
        norm_done = sem("norm_done")
        x1_kept = sem("x1_kept")
        t_done = sem("t_done")
        t_copied = sem("t_copied")
        h_done = sem("h_done")
        u_done = sem("u_done")
        r_done = sem("r_done")
        q_done = sem("q_done")
        hi_done = sem("hi_done")
        v_done = sem("v_done")
        k_part = sem("k_part")
        k_row = sem("k_row")
        k_one = sem("k_one")
        k_bcast = sem("k_bcast")
        p_done = sem("p_done")
        mean_in = sem("mean_in")
        mean_mm = sem("mean_mm")
        mean_done = sem("mean_done")
        y_done = sem("y_done")
        stored = [sem(f"stored{s}") for s in range(FIN)]
        far_done = sem("far_done")
        far_sum = sem("far_sum")
        flag_done = sem("flag_done")
        g_w = sem("g_w")
        g_x = sem("g_x")
        g_t = sem("g_t")
        g_tc = sem("g_tc")
        g_f = sem("g_f")
        g_fc = sem("g_fc")
        g_h = sem("g_h")
        g_hc = sem("g_hc")
        g_adj = sem("g_adj")
        g_own = sem("g_own")
        g_e = sem("g_e")
        g_exp = sem("g_exp")
        g_turn = sem("g_turn")
        g_tcopy = sem("g_tcopy")
        g_acc = sem("g_acc")
        g_var = sem("g_var")
        g_pow = sem("g_pow")
        g_row = sem("g_row")
        g_stored = sem("g_stored")

        BLOCKS = [HB, HB, HB, QB, QB]
        COL0 = [0, HALF, 0, HALF, HALF + QB * P]
        BANK0 = [0, 0, 0, 0, BANKS // 2]
        NBANKS = [-(-n // PER_BANK) for n in BLOCKS]
        BY_DVE = [BANKS // 2, BANKS // 2, BANKS // 2, 1, 1]
        SHARE = BY_DVE[0] * PER_BANK
        TURNS = TILES // RING

        def tiles_used(eng, t):
            if t.w or t.base >= RING:
                eng.wait_ge(tile_used, t.n - RING + 1)

        def slot_free1(eng, t):
            if t.w == L1 and t.base < RING:
                eng.wait_ge(masked, t.n - RING + 1)
            else:
                eng.wait_ge(tile_used, t.n - RING + 1)

        def adj_arrived(eng, t):
            eng.wait_ge(adj_in[t.slot], 16 * (t.w * TURNS + t.base // RING + t.i + 1))

        def scores_by_act(t):
            return t.slot == RING - 1

        def cols_of(w):
            return slice(COL0[w], COL0[w] + BLOCKS[w] * P)

        plan0 = {e: {} for e in ("pe", "act", "dve")}
        plan1 = {e: {} for e in ("pe", "act", "dve")}

        def at(plan, tile, stage, g):
            plan.setdefault(tile, []).append((stage, g))

        for k in range(A_GROUPS):
            b0 = 1 + 6 * k
            at(plan0["dve"], b0, "variance", k)
            at(plan0["pe"], b0 + 2, "turn", k)
            at(plan0["act"], b0 + 5, "copy_T", k)
            at(plan0["pe"], b0 + 4, "project", k)
            at(plan0["dve"], b0 + 6, "powers", k)
            at(plan0["act"], b0 + 8, "exp_r", k)
            at(plan0["dve"], b0 + 8, "parts", k)
            at(plan0["act"], b0 + 10, "high", k)
            at(plan0["dve"], b0 + 10, "low", k)
            b1, g = 3 * k, A_GROUPS + k
            at(plan1["dve"], b1, "variance", g)
            at(plan1["dve"], b1 + 1, "norm", g)
            at(plan1["pe"], b1 + 1, "turn", g)
            at(plan1["act"], b1 + 4, "copy_T", g)
            at(plan1["pe"], b1 + 3, "project", g)
            at(plan1["dve"], b1 + 5, "powers", g)
            at(plan1["act"], b1 + 6, "exp_r", g)
            at(plan1["dve"], b1 + 6, "parts", g)
            at(plan1["act"], b1 + 7, "high", g)
            at(plan1["dve"], b1 + 7, "low", g)
        for p in (plan0["dve"],):
            for tile in p:
                p[tile].sort(key=lambda s: s[1])

        block = ctx.enter_context(nc.Block())

        @block.sync
        def _(sp):
            for c in range(4):
                sp.dma_start(xT_sb[:, c * 1024:(c + 1) * 1024],
                             xT[:, c * 1024:(c + 1) * 1024]).then_inc(xT_in[c], 16)

            def load(t):
                tiles_used(sp, t)
                sp.dma_start(adj_ring[:, t.slot, :],
                             adjT[t.w, bass.ds(t.jt, 1), :, :].rearrange("a p n -> p (a n)"))\
                  .then_inc(adj_in[t.slot], 16)

            for jt in range(RING):
                load(Tile(0, jt))
            sp.dma_start(xs[:, :, :], x.rearrange("(t p) d -> p t d", p=P)).then_inc(x_in, 16)
            turns(sp, 0, RING, TURNS - 1, load)
            turns(sp, 1, 0, TURNS, load)

            def load_again(t):
                if t.w == L1 and t.base < RING and isinstance(t.i, int):
                    sp.wait_ge(tile_used, L1 * TILES - RING + t.again_slot + 1)
                else:
                    sp.wait_ge(scaled_v, (t.w - L1) * RESIDENT + t.half - 1)
                off = COL0[t.w] % HALF
                cols = BLOCKS[t.w] * P
                sp.dma_start(adj_ring[:, t.again_slot, 0:cols],
                             adjT[COL0[t.w] // HALF, bass.ds(t.jt, 1), :, off:off + cols]
                             .rearrange("a p n -> p (a n)")).then_inc(again_in[t.again_slot], 16)

            def odd(t):
                if not t.resident:
                    load_again(t)

            def store(g):
                sp.wait_ge(norm_done, GROUPS + g + 1)
                sp.dma_start(out.rearrange("(t p) d -> p t d", p=P)[:, g * GROUP:(g + 1) * GROUP, :],
                             fin[:, g % FIN * GROUP:(g % FIN + 1) * GROUP, :]).then_inc(stored[g % FIN], 16)

            for jt in range(RING):
                odd(Tile(L1, jt))
            turns(sp, L1, RING, TURNS - 1, odd)
            turns(sp, L1 + 1, 0, TURNS, odd)
            for g in range(4):
                store(g)
            turns(sp, L1 + 2, 0, TURNS, odd)
            for g in range(4, GROUPS):
                store(g)
            for s in range(FIN):
                sp.wait_ge(stored[s], 16 * (GROUPS // FIN))
            sp.wait_ge(flag_done, 2)
            far_nodes = sp.value_load(flag[0:1, 0:1], min_val=0, max_val=N)
            with sp.If(far_nodes > 0):
                with sp.Fori(0, TILES) as t:
                    sp.wait_ge(g_e, t * 3 + 2)
                    sp.dma_start(adj_row, adj.rearrange("(t p) n -> t p n", p=P)[bass.ds(t, 1), :, :]
                                 .rearrange("a p n -> p (a n)")).then_inc(g_adj, 16)
                    sp.wait_ge(g_row, t + 1)
                    sp.dma_start(out.rearrange("(t p) d -> t p d", p=P)[bass.ds(t, 1), :, :]
                                 .rearrange("a p d -> p (a d)"), g_out[:, :]).then_inc(g_stored, 16)

        @block.gpsimd
        def _(pool):
            pool.memset(ones[:, :], 1.0).then_inc(consts, 1)
            pool.memset(zeros[:, :], 0.0).then_inc(consts, 1)
            pool.memset(fe[:, :, :], 1.0).then_inc(consts, 1)
            pool.memset(half_neg[:, :], -0.5).then_inc(consts, 1)
            pool.wait_ge(x_in, 16)
            pool.wait_ge(w_in, 16)
            pool.tensor_tensor(xs[:, :, :], xs[:, :, :],
                               bb.unsqueeze(1).to_broadcast([P, TILES, D]), ALU.add).then_inc(xb_done, 1)
            pool.wait_ge(consts, 4)
            pool.wait_ge(xb_done, 1)

            def add_share(w):
                pool.wait_ge(freed_a, (w + 1) * (BANKS - BY_DVE[w]))
                ys = xs[:, w * HB + SHARE:(w + 1) * HB, :]
                pool.tensor_tensor(ys, ys, read0[:, 0:HB - SHARE, :], ALU.add).then_inc(y0_added, 1)

            def rsqrt(c, k=0):
                c.step(pool.tensor_tensor(rstd[k][:, :], veps[k][:, :], half_neg[:, :], ALU.pow))

            def keep(g):
                pool.wait_ge(norm_done, g + 1)
                pool.tensor_copy(xs[:, g * GROUP:(g + 1) * GROUP, :], x1n[:, :, :]).then_inc(x1_kept, 1)

            add_share(0)
            for g in range(GROUPS):
                if g == A_GROUPS:
                    add_share(1)
                pool.wait_ge(var_done, g + 1)
                rsqrt(Chain(pool, rstd_done, g, 1))
                if g < A_GROUPS:
                    if g:
                        pool.wait_ge(t_done, g)
                        pool.wait_ge(x1_kept, g)
                    for k in range(GROUP):
                        ins = pool.tensor_scalar(x1n[:, k, :], xs[:, g * GROUP + k, :], mv[0][:, k, 0:1],
                                                 rstd[0][:, k:k + 1], ALU.subtract, ALU.mult)
                    ins.then_inc(norm_done, 1)
                keep(g)

            def finish(g):
                k = int(g == GROUPS - 1)
                pool.wait_ge(y_done, g + 1)
                if FIN <= g < GROUPS - 2:
                    pool.wait_ge(stored[g % FIN], 16 * (g // FIN))
                rsqrt(Chain(pool, rstd_done, GROUPS + g, 1), k)
                if g < GROUPS - 2:
                    for n in range(GROUP):
                        ins = pool.tensor_scalar(fin[:, g % FIN * GROUP + n, :],
                                                 obuf[:, (g * GROUP if g < 4 else (g - 4) * GROUP) + n, :],
                                                 mv[0][:, n, 0:1], rstd[0][:, n:n + 1], ALU.subtract, ALU.mult)
                    ins.then_inc(norm_done, 1)

            for g in range(GROUPS):
                finish(g)
            pool.wait_ge(flag_done, 2)
            far_nodes = pool.value_load(flag[0:1, 0:1], min_val=0, max_val=N)
            with pool.If(far_nodes > 0):
                with pool.Fori(0, TILES) as t:
                    pool.wait_ge(g_var, t + 1)
                    pool.tensor_tensor(rstd[0][:, :], veps[0][:, :], half_neg[:, :], ALU.pow).then_inc(g_pow, 1)

        @block.scalar
        def _(act):
            act.dma_start(weights[:, :], weights_d).then_inc(w_in, 16)

            def copy_el(c):
                act.wait_ge(el_done, c + 1)
                act.activation(elb[c // 4][:, c % 4 * BANK:(c % 4 + 1) * BANK], el_bank(c), ACT.Copy)\
                   .then_inc(el_copied, 1)

            def exp_F(a):
                t0 = 3 * a
                n = min(3, TILES - t0)
                act.wait_ge(elr_copied, a + 1)
                act.activation(Fj[:, t0:t0 + n], elr[:, t0:t0 + n, 1], ACT.Exp, scale=SLOPE).then_inc(F_done, 1)

            def tile0(t):
                s = t.slot
                if t.resident:
                    adj_arrived(act, t)
                    act.activation(signs[:, bass.ds(t.half, 1), COL0[t.w]:COL0[t.w] + HALF]
                                   .rearrange("p a n -> p (a n)"), adj_ring[:, s, :], ACT.Sign)
                if scores_by_act(t):
                    if t.n_after_ring:
                        act.wait_ge(masked, t.n - RING + 1)
                    act.activation(pair[:, s, :], elb[t.w], ACT.Relu, bias=elr[:, bass.ds(t.jt, 1), 1])\
                       .then_inc(scored_a, 1)
                    act.wait_ge(scored_a, t.w * TURNS + t.base // RING + t.i + 1)
                else:
                    act.wait_ge(scored_v, (t.w * TURNS + t.base // RING + t.i) * (RING - 1) + s + 1)
                act.activation(pair[:, s, :], pair[:, s, :], ACT.Exp, scale=1.0 - SLOPE).then_inc(exped, 1)

            def read_out(w):
                act.wait_ge(coef_done, w + 1)
                if w == 1:
                    act.wait_ge(y0_added, 1)
                if w > L1:
                    act.wait_ge(norm_done, GROUPS + 4)
                first = BY_DVE[w] * PER_BANK
                for n in range(first, BLOCKS[w]):
                    dst = read0[:, n - SHARE, :] if w < L1 else obuf[:, (QB if w == L1 + 2 else 0) + n, :]
                    ins = act.activation(dst, acc_of(n, BANK0[w])[:, 0:D], ACT.Relu if w >= L1 else ACT.Copy,
                                         scale=coef[:, n:n + 1])
                    if n % PER_BANK == PER_BANK - 1 or n == BLOCKS[w] - 1:
                        ins.then_inc(freed_a, 1)

            def copy_T(g):
                act.wait_ge(t_done, g + 1)
                if g:
                    act.wait_ge(h_done, g)
                act.activation(x1T[:, :], ps_t[:, :], ACT.Identity,
                               accum_out=xsum[:, g:g + 1]).then_inc(t_copied, 1)

            def exp_r(g):
                act.wait_ge(u_done, g + 1)
                act.activation(rj[:, :], u2[:, :], ACT.Exp).then_inc(r_done, 1)

            def high(g):
                act.wait_ge(q_done, g + 1)
                for k in range(GROUP):
                    ins = act.activation(V_v[:, g * GROUP + k, 0:D], ps_h[:, k * P:(k + 1) * P],
                                         ACT.Copy, scale=q[:, k:k + 1])
                ins.then_inc(hi_done, 1)

            stages = {"copy_T": copy_T, "exp_r": exp_r, "high": high}

            def scale(t):
                if not t.resident:
                    return
                slot_free1(act, t)
                act.activation(pair16[:, t.slot, 0:BLOCKS[t.w] * P],
                               signs[:, bass.ds(t.half, 1), cols_of(t.w)].rearrange("p a n -> p (a n)"),
                               ACT.Relu, scale=pj_f[:, bass.ds(t.jt, 1)]).then_inc(scaled_a, 1)

            for c in range(4):
                copy_el(c)
            exp_F(0)
            for jt in range(RING):
                tile0(Tile(0, jt))
                for a in [[1, 2], [3, 4], [5, 6, 7], [8, 9, 10]][jt]:
                    exp_F(a)
            for c in range(4, 8):
                copy_el(c)
            for h in range(2):
                act.activation(fe[:, h, 0:HB], elr[:, h * HB:(h + 1) * HB, 0], ACT.Exp, scale=SLOPE)\
                   .then_inc(fe_done, 1)
            turns(act, 0, RING, TURNS - 1, tile0)
            for jt in range(TILES):
                if jt == 2:
                    read_out(0)
                for stage, g in plan0["act"].get(jt, []):
                    stages[stage](g)
                tile0(Tile(1, jt))

            act.wait_ge(p_done, 1)
            for jt in range(HB + 1):
                if jt == 3:
                    read_out(1)
                for stage, g in plan1["act"].get(jt, []):
                    stages[stage](g)
                if jt < HB:
                    scale(Tile(L1, jt))
            turns(act, L1, HB, A_GROUPS, scale, lambda i: act.wait_ge(p_done, i + 2))
            for w in (L1 + 1, L1 + 2):
                for jt in range(RING):
                    scale(Tile(w, jt))
                read_out(w - 1)
                turns(act, w, RING, TURNS - 1, scale)
            read_out(L1 + 2)
            act.wait_ge(flag_done, 2)
            far_nodes = act.value_load(flag[0:1, 0:1], min_val=0, max_val=N)
            with act.If(far_nodes > 0):
                with act.Fori(0, GROUPS) as g:
                    act.wait_ge(g_t, g + 1)
                    act.activation(x1T[:, :], ps_t[:, :], ACT.Copy).then_inc(g_tc, 1)
                    act.wait_ge(g_f, g + 1)
                    act.activation(fb[:, bass.ds(g * BANK, BANK)], acc[:, 0, :], ACT.Copy).then_inc(g_fc, 1)
                    act.wait_ge(g_h, g + 1)
                    act.activation(hfull[:, bass.ds(g * GROUP, GROUP), :],
                                   acc[:, 1, :].rearrange("p (k d) -> p k d", d=D), ACT.Copy).then_inc(g_hc, 1)
                with act.Fori(0, TILES) as t:
                    act.wait_ge(g_e, t * 3 + 5)
                    act.activation(e_row, e_row, ACT.Exp, bias=g_max[:, 0:1], accum_out=g_sum[:, 0:1])\
                       .then_inc(g_exp, 1)
                    for c in range(GROUPS):
                        act.wait_ge(g_turn, t * GROUPS + c + 1)
                        act.activation(t_row[:, c % 2 * BANK:(c % 2 + 1) * BANK], small[c % 2][:, :], ACT.Copy)\
                           .then_inc(g_tcopy, 1)

        @block.vector
        def _(dve):
            dve.wait_ge(wa_done, 1)
            dve.tensor_copy(w0[:, D:D + 2], ps_t[:, 0:2]).then_inc(wa_copied, 1)
            dve.tensor_copy(wad[:, :], ps_t[:, 8:9]).then_inc(wa_copied, 1)
            dve.wait_ge(wa_copied, 2)
            dve.wait_ge(consts, 3)
            dve.tensor_scalar(walb[:, :], ones[:, :], w0[:, D:D + 1], None, ALU.mult).then_inc(wa_copied, 1)
            dve.wait_ge(wa_done, 2)
            dve.tensor_copy(wf[:, :], ps_t[:, 16:17]).then_inc(wa_copied, 1)

            def copy_elr(a):
                t0 = 3 * a
                n = min(3, TILES - t0)
                ps = small[a % 2][:, 0:n * (D + 2)].rearrange("p (t c) -> p t c", c=D + 2)
                dve.wait_ge(h0_done, a + 1)
                dve.tensor_copy(elr[:, t0:t0 + n, :], ps[:, :, D:D + 2]).then_inc(elr_copied, 1)

            def weigh_h(a):
                t0 = 3 * a
                n = min(3, TILES - t0)
                ps = small[a % 2][:, 0:n * (D + 2)].rearrange("p (t c) -> p t c", c=D + 2)
                dve.wait_ge(F_done, a + 1)
                dve.tensor_tensor(haug[:, t0:t0 + n, 0:D], ps[:, :, 0:D],
                                  Fj[:, t0:t0 + n].unsqueeze(2).to_broadcast([P, n, D]), ALU.mult)
                dve.tensor_copy(haug[:, t0:t0 + n, D], Fj[:, t0:t0 + n]).then_inc(haug_done, 1)

            def score(t):
                if scores_by_act(t) or t.w == L1:
                    return
                if t.n_after_ring:
                    dve.wait_ge(masked, t.n - RING + 1)
                dve.tensor_scalar(pair[:, t.slot, :], elb[t.w], elr[:, bass.ds(t.jt, 1), 1], 0.0,
                                  ALU.add, ALU.max).then_inc(scored_v, 1)

            def mask(t):
                s = t.slot
                dve.wait_ge(exped, t.n + 1)
                adj_arrived(dve, t)
                dve.scalar_tensor_tensor(out=adj_ring[:, s, :], in0=adj_ring[:, s, :], scalar=0.0,
                                         in1=pair[:, s, :], op0=ALU.not_equal, op1=ALU.mult)\
                   .then_inc(masked, 1)

            def tile0(t):
                score(t.ahead(AHEAD))
                mask(t)

            def read_out0(w):
                c = Chain(dve, own["y"], w, 3)
                dve.wait_ge(tile_used, TILES * (w + 1))
                if w:
                    dve.wait_ge(freed_a, BANKS - BY_DVE[0])
                c.step(dve.tensor_tensor(by_bank(den, BANKS), den_of(0, BANKS), by_bank(fe[:, w, :], BANKS),
                                         ALU.mult))
                c.step(dve.tensor_scalar(den[:, :], den[:, :], TINY, None, ALU.max))
                c.step(dve.reciprocal(den[:, :], den[:, :]))
                dve.tensor_tensor(coef[:, :], den[:, :], fe[:, w, :], ALU.mult).then_inc(coef_done, 1)
                dve.wait_ge(coef_done, w + 1)
                for n in range(SHARE):
                    y = xs[:, w * HB + n, :]
                    ins = dve.scalar_tensor_tensor(out=y, in0=acc_of(n)[:, 0:D], scalar=coef[:, n:n + 1],
                                                   in1=y, op0=ALU.mult, op1=ALU.add)
                    if n % PER_BANK == PER_BANK - 1:
                        ins.then_inc(freed_v, 1)
                c.end()

            def moments(c, rows, k=0):
                dve.memset(scratch[:, 0:1], 0.0)
                for n in range(GROUP):
                    ins = dve.bn_stats(stats[:, n, :], rows(n))
                c.step(ins)
                dve.memset(scratch[:, 1:2], 0.0)
                for n in range(GROUP):
                    ins = dve.bn_aggr(mv[k][:, n, :], stats[:, n, :])
                c.step(ins)

            def variance(g):
                c = Chain(dve, own["var"], g, 2)
                if g:
                    dve.wait_ge(norm_done, g)
                if g % A_GROUPS == 0:
                    dve.wait_ge(freed_v, (g // A_GROUPS + 1) * BY_DVE[0])
                if g % A_GROUPS == SHARE // GROUP:
                    dve.wait_ge(y0_added, g // A_GROUPS + 1)
                moments(c, lambda n: xs[:, g * GROUP + n, :])
                dve.tensor_scalar(veps[0][:, :], mv[0][:, :, 1], EPS, None, ALU.add).then_inc(var_done, 1)
                c.end()

            def norm(g):
                dve.wait_ge(rstd_done, g + 1)
                dve.wait_ge(t_done, g)
                dve.wait_ge(x1_kept, g)
                for k in range(GROUP):
                    ins = dve.tensor_scalar(x1n[:, k, :], xs[:, g * GROUP + k, :], mv[0][:, k, 0:1],
                                            rstd[0][:, k:k + 1], ALU.subtract, ALU.mult)
                ins.then_inc(norm_done, 1)

            def powers(g):
                c = Chain(dve, own["pow"], g, 6)
                cols = slice(g * GROUP, (g + 1) * GROUP)
                dve.wait_ge(h_done, g + 1)
                c.step(dve.tensor_scalar(k_int[:, :], ps_t[:, 0:GROUP], LOG2E, None, ALU.mult))
                c.step(dve.scalar_tensor_tensor(out=u1[:, :], in0=k_int[:, :], scalar=-LN2_HI,
                                                in1=ps_t[:, 0:GROUP], op0=ALU.mult, op1=ALU.add))
                dve.scalar_tensor_tensor(out=u2[:, :], in0=k_int[:, :], scalar=-LN2_LO, in1=u1[:, :],
                                         op0=ALU.mult, op1=ALU.add).then_inc(u_done, 1)
                dve.tensor_copy(kf[:, cols], k_int[:, :])
                c.step(dve.tensor_reduce(hmax[:, :], ps_h[:, :].rearrange("p (k d) -> p k d", d=D),
                                         AX.X, ALU.max, apply_absolute_value=True))
                c.step(dve.tensor_scalar(hmax1[:, :], hmax[:, :], 1.0, None, ALU.max))
                c.step(dve.tensor_scalar(hexp[:, :], hmax1[:, :].bitcast(I32), EXP_MASK, None, ALU.bitwise_and))
                dve.tensor_scalar(hef[:, cols], hexp[:, :], 1.0 / EXPONENT, None, ALU.mult)
                c.step(dve.tensor_scalar(hinv[:, :], hexp[:, :], -1.0, float((254 + V_SCALE) * EXPONENT),
                                         ALU.mult, ALU.add))
                c.end()
                if g >= A_GROUPS:
                    mask_powers(1 + g - A_GROUPS, g * GROUP, GROUP)

            def parts(g):
                c = Chain(dve, own["parts"], g, 2)
                rows = V_v[:, g * GROUP:(g + 1) * GROUP, :]
                dve.wait_ge(r_done, g + 1)
                dve.tensor_tensor(q[:, :], rj[:, :], hinv[:, :].bitcast(F32), ALU.mult).then_inc(q_done, 1)
                dve.wait_ge(q_done, g + 1)
                c.step(dve.tensor_copy(rows[:, :, D], q[:, :]))
                c.step(dve.tensor_tensor(rows[:, :, DV + D], q[:, :], rows[:, :, D], ALU.subtract))
                c.end()

            def low(g):
                dve.wait_ge(hi_done, g + 1)
                for k in range(GROUP):
                    row = V_v[:, g * GROUP + k, :]
                    ins = dve.scalar_tensor_tensor(out=row[:, DV:DV + D], in0=ps_h[:, k * P:(k + 1) * P],
                                                   scalar=q[:, k:k + 1], in1=row[:, 0:D],
                                                   op0=ALU.mult, op1=ALU.subtract)
                ins.then_inc(v_done, 1)

            def mask_powers(call, t0, n):
                c = Chain(dve, own["mask"], call, 2)
                cols = slice(t0, t0 + n)
                c.step(dve.scalar_tensor_tensor(out=te[:, cols], in0=kf[:, cols], scalar=Kb[:, 0:1],
                                                in1=hef[:, cols], op0=ALU.subtract, op1=ALU.add))
                c.step(dve.tensor_scalar(tec[:, cols], te[:, cols], 254.0, 1.0, ALU.min, ALU.max))
                dve.tensor_scalar(pj[:, cols], tec[:, cols], float(EXPONENT), None, ALU.mult)\
                   .then_inc(p_done, 1)
                c.end()

            stages = {"variance": variance, "norm": norm, "powers": powers, "parts": parts, "low": low}

            copy_elr(0)
            dve.wait_ge(elr_copied, 1)
            dve.wait_ge(el_copied, 4)
            score(Tile(0, 0))
            score(Tile(0, 1))
            weigh_h(0)
            for jt in range(RING):
                for a in [[1, 2], [3, 4], [5, 6, 7], [8, 9, 10]][jt]:
                    copy_elr(a)
                    weigh_h(a)
                tile0(Tile(0, jt))
            dve.wait_ge(elr_copied, 11)
            turns(dve, 0, RING, TURNS - 2, tile0)
            for jt in range(TILES - RING, TILES):
                if jt == TILES - AHEAD:
                    dve.wait_ge(el_copied, N // BANK)
                tile0(Tile(0, jt))
            dve.wait_ge(fe_done, 2)
            dve.wait_ge(xb_done, 1)
            for jt in range(TILES):
                if jt == 1:
                    read_out0(0)
                for stage, g in plan0["dve"].get(jt, []):
                    stages[stage](g)
                if jt == 26:
                    dve.wait_ge(u_done, A_GROUPS)
                    dve.tensor_reduce(kpart[:, :], kf[:, 0:HB], AX.X, ALU.max).then_inc(k_part, 1)
                if jt == 30:
                    dve.wait_ge(k_row, 1)
                    dve.tensor_reduce(k1[:, :], ps_t[0:1, 0:P], AX.X, ALU.max).then_inc(k_one, 1)
                tile0(Tile(1, jt))
            c = Chain(dve, own["k"], 0, 1)
            dve.wait_ge(k_bcast, 1)
            c.step(dve.tensor_copy(Kb[:, :], ps_t[:, 256:257]))
            mask_powers(0, 0, HB)
            dve.wait_ge(p_done, 1)

            def scale(t):
                if t.resident:
                    return
                slot_free1(dve, t)
                s, cols = t.again_slot, BLOCKS[t.w] * P
                dve.wait_ge(again_in[s], 16 * ((t.w - L1) * TURNS + t.base // RING + t.i + 1))
                dve.tensor_scalar(pair16[:, t.slot, 0:cols], adj_ring[:, s, 0:cols], 0.0,
                                  pj_f[:, bass.ds(t.jt, 1)], ALU.is_gt, ALU.mult).then_inc(scaled_v, 1)

            scale(Tile(L1, 1))
            scale(Tile(L1, 3))
            read_out0(1)
            for jt in range(HB + 1):
                for stage, g in plan1["dve"].get(jt, []):
                    stages[stage](g)
                if RING <= jt < HB:
                    scale(Tile(L1, jt))
            dve.wait_ge(t_copied, GROUPS)
            dve.tensor_reduce(xtot[:, :], xsum[:, :], AX.X, ALU.add).then_inc(mean_in, 1)
            dve.wait_ge(mean_in, 1)
            dve.tensor_scalar(xmb[:, :], ones[:, :], xtot[:, 0:1], 1.0 / N, ALU.mult, ALU.mult)\
               .then_inc(mean_in, 1)
            turns(dve, L1, HB, A_GROUPS, scale, lambda i: dve.wait_ge(p_done, i + 2))
            dve.wait_ge(x1_kept, GROUPS)
            dve.wait_ge(mean_mm, 1)
            dve.tensor_scalar(hmean[:, :], ps_t[:, 0:P], 0.0, None, ALU.max).then_inc(mean_done, 1)
            dve.wait_ge(mean_done, 1)
            c = Chain(dve, own["far"], 0, 3)
            dve.tensor_scalar(far[:, 0, :], te[:, :], TE_HIGH, None, ALU.is_gt)
            c.step(dve.tensor_scalar(far[:, 1, :], te[:, :], TE_LOW, None, ALU.is_lt))
            c.step(dve.tensor_reduce(far_any[:, :], far[:, :, :], AX.XY, ALU.add))
            dve.sem_inc(far_done, 1)

            def read_out1(w):
                c = Chain(dve, own["coef"], w - L1, 2)
                nb = NBANKS[w]
                dve.wait_ge(tile_used, TILES * (w + 1))
                dve.wait_ge(freed_a, sum(NBANKS[v] - BY_DVE[v] for v in range(w)))
                c.step(dve.tensor_scalar(by_bank(none, nb), den_of(BANK0[w], nb), 0.0, None, ALU.is_equal))
                c.step(dve.tensor_tensor(by_bank(den, nb), den_of(BANK0[w], nb), by_bank(none, nb), ALU.add))
                dve.reciprocal(by_bank(coef, nb), by_bank(den, nb)).then_inc(coef_done, 1)
                dve.wait_ge(coef_done, w + 1)
                if w > L1:
                    dve.wait_ge(norm_done, GROUPS + 4)
                for n in range(BY_DVE[w] * PER_BANK):
                    ins = dve.tensor_scalar(obuf[:, (QB if w == L1 + 2 else 0) + n, :],
                                            acc_of(n, BANK0[w])[:, 0:D], coef[:, n:n + 1], 0.0,
                                            ALU.mult, ALU.max)
                    if n % PER_BANK == PER_BANK - 1:
                        ins.then_inc(freed_v, 1)
                c.end()

            def row_of(v, n):
                return v[:, bass.ds(n, 1), :].rearrange("p a d -> p (a d)")

            def last_y(g, n0, o0):
                c = Chain(dve, own["last"], g, 4)
                k = int(isinstance(g, int) and g == GROUPS - 1)
                for n in range(GROUP):
                    y = row_of(obuf, o0 + n)
                    ins = dve.scalar_tensor_tensor(out=y, in0=hmean[:, :], scalar=none[:, bass.ds(n0 + n, 1)],
                                                   in1=y, op0=ALU.mult, op1=ALU.add)
                c.step(ins)
                c.step(dve.tensor_tensor(obuf[:, bass.ds(o0, GROUP), :], obuf[:, bass.ds(o0, GROUP), :],
                                         xs[:, bass.ds(g * GROUP, GROUP), :], ALU.add))
                if not k:
                    dve.wait_ge(norm_done, g + GROUPS)
                moments(c, lambda n: row_of(obuf, o0 + n), k)
                dve.tensor_scalar(veps[k][:, :], mv[k][:, :, 1], EPS, None, ALU.add).then_inc(y_done, 1)
                c.end()

            def finish(g):
                k = int(g == GROUPS - 1)
                dve.wait_ge(rstd_done, GROUPS + g + 1)
                dve.wait_ge(stored[g % FIN], 16 * (g // FIN))
                for n in range(GROUP):
                    ins = dve.tensor_scalar(fin[:, g % FIN * GROUP + n, :], obuf[:, (g - 4) * GROUP + n, :],
                                            mv[k][:, n, 0:1], rstd[k][:, n:n + 1], ALU.subtract, ALU.mult)
                ins.then_inc(norm_done, 1)

            for w, first, groups in ((L1 + 1, 0, 4), (L1 + 2, 4, 2)):
                for jt in range(RING):
                    scale(Tile(w, jt))
                read_out1(w - 1)
                dve.wait_ge(freed_v, sum(BY_DVE[:w]))
                dve.wait_ge(freed_a, sum(NBANKS[v] - BY_DVE[v] for v in range(w)))
                turns(dve, w, RING, groups, scale, lambda i: last_y(i + first, i * GROUP, i * GROUP))
                turns(dve, w, RING + RING * groups, TURNS - 1 - groups, scale)
            read_out1(L1 + 2)
            dve.wait_ge(freed_v, sum(BY_DVE))
            for g in (6, 7):
                dve.wait_ge(freed_a, sum(n - v for n, v in zip(NBANKS, BY_DVE)) - (7 - g))
                last_y(g, (g - 6) * GROUP, QB + (g - 6) * GROUP)
            for g in (6, 7):
                finish(g)
            dve.wait_ge(far_sum, 1)
            dve.tensor_copy(flag[:, :], ps_t[0:1, 256:257]).then_inc(flag_done, 1)
            dve.wait_ge(flag_done, 1)
            for s in range(FIN):
                dve.wait_ge(stored[s], 16 * (GROUPS // FIN))
            dve.sem_inc(flag_done, 1)
            far_nodes = dve.value_load(flag[0:1, 0:1], min_val=0, max_val=N)
            with dve.If(far_nodes > 0):
                dve.tensor_scalar(wfb[:, :], ones[:, :], wf[:, 0:1], None, ALU.mult).then_inc(g_w, 1)
                dve.tensor_copy(x1n[:, :, :], xs[:, 0:GROUP, :]).then_inc(g_x, 1)
                with dve.Fori(0, GROUPS - 1) as g:
                    dve.wait_ge(g_hc, g + 1)
                    dve.tensor_copy(x1n[:, :, :], xs[:, bass.ds(g * GROUP + GROUP, GROUP), :]).then_inc(g_x, 1)
                dve.wait_ge(g_hc, GROUPS)
                dve.memset(scratch[:, :], 0.0).then_inc(g_e, 1)
                dve.wait_ge(g_e, 1)
                dve.memset(scratch[:, :], 0.0).then_inc(g_e, 1)
                dve.sem_inc(g_stored, 16)
                with dve.Fori(0, TILES) as t:
                    c = Chain(dve, g_own, t, 6)
                    dve.wait_ge(g_adj, t * 16 + 16)
                    dve.wait_ge(g_stored, t * 16 + 16)
                    dve.scalar_tensor_tensor(out=e_row, in0=adj_row, scalar=0.0, in1=fb, op0=ALU.is_gt, op1=ALU.mult)
                    c.step(dve.tensor_scalar(t_row, adj_row, 0.0, NEG_INF, ALU.is_le, ALU.mult))
                    dve.tensor_tensor(e_row, e_row, t_row, ALU.add).then_inc(g_e, 1)
                    dve.wait_ge(g_e, t * 3 + 3)
                    dve.tensor_reduce(g_max[:, :], e_row, AX.X, ALU.max, negate=True).then_inc(g_e, 1)
                    dve.wait_ge(g_e, t * 3 + 4)
                    dve.memset(scratch[:, 0:1], 0.0).then_inc(g_e, 1)
                    dve.wait_ge(g_exp, t + 1)
                    dve.wait_ge(g_acc, t + 1)
                    c.step(dve.reciprocal(g_rec[:, :], g_sum[:, :]))
                    c.step(dve.tensor_scalar(g_y[:, :], acc[:, 0, 0:D], g_rec[:, 0:1], 0.0, ALU.mult, ALU.max))
                    c.step(dve.tensor_tensor(g_y[:, :], g_y[:, :], row_of(xs, t), ALU.add))
                    dve.memset(scratch[:, 0:1], 0.0)
                    c.step(dve.bn_stats(stats[:, 0, :], g_y[:, :]))
                    dve.memset(scratch[:, 1:2], 0.0)
                    c.step(dve.bn_aggr(mv[0][:, 0, :], stats[:, 0, :]))
                    dve.tensor_scalar(veps[0][:, :], mv[0][:, :, 1], EPS, None, ALU.add).then_inc(g_var, 1)
                    dve.wait_ge(g_pow, t + 1)
                    dve.tensor_scalar(g_out[:, :], g_y[:, :], mv[0][:, 0, 0:1], rstd[0][:, 0:1],
                                      ALU.subtract, ALU.mult).then_inc(g_row, 1)
                    c.end()
                dve.wait_ge(g_stored, TILES * 16 + 16)

        @block.tensor
        def _(pe):
            pe.wait_ge(w_in, 16)
            pe.matmul(ps_t[:, 0:2], w0T, alr, start=True, stop=True)
            pe.matmul(ps_t[:, 8:9], waT, adst, start=True, stop=True).then_inc(wa_done, 1)
            pe.wait_ge(wa_copied, 2)
            pe.matmul(ps_t[:, 16:17], w1T_sb, wad[:, :], start=True, stop=True).then_inc(wa_done, 1)
            pe.wait_ge(wa_copied, 3)

            def el_rows(c):
                if c == 4:
                    pe.wait_ge(haug_done, 11)
                if c >= 6:
                    pe.wait_ge(el_copied, c - 1)
                pe.matmul(el_bank(c), walb[:, :], xT_sb[:, c * BANK:(c + 1) * BANK],
                          start=True, stop=True).then_inc(el_done, 1)

            def h_tiles(a):
                if a >= 2:
                    pe.wait_ge(haug_done, a - 1)
                t0 = 3 * a
                for n in range(min(3, TILES - t0)):
                    if (t0 + n) % 8 == 0:
                        pe.wait_ge(xT_in[(t0 + n) // 8], 16)
                    ins = pe.matmul(small[a % 2][:, n * (D + 2):(n + 1) * (D + 2)],
                                    xT_sb[:, (t0 + n) * P:(t0 + n + 1) * P], w0, start=True, stop=True)
                ins.then_inc(h0_done, 1)

            pe.wait_ge(wa_copied, 4)
            pe.wait_ge(xT_in[0], 16)
            el_rows(0)
            el_rows(1)
            pe.wait_ge(xT_in[1], 16)
            el_rows(2)
            el_rows(3)
            for a in range(11):
                h_tiles(a)

            def clear(bank):
                pe.matmul(acc[:, bank, 0:PER_BANK * DA], zeros[:, 0:P], zeros[:, :], start=True, stop=False,
                          skip_group_check=True)

            def bank_ready(w, bank):
                if w == 0:
                    pe.wait_ge(el_copied, 4)
                else:
                    half = BANKS // 2
                    at = min(w, SWEEPS0 + 1) - 1
                    pe.wait_ge(freed_v if bank < half else freed_a, at * half + bank % half + 1)

            def tile0(t):
                pe.wait_ge(masked, t.n + 1)
                for n in range(HB):
                    if t.first and n % PER_BANK == 0:
                        bank_ready(t.w, n // PER_BANK)
                        clear(n // PER_BANK)
                    ins = pe.matmul(acc_of(n), adj_ring[:, t.slot, n * P:(n + 1) * P],
                                    haug[:, bass.ds(t.jt, 1), :].rearrange("p a d -> p (a d)"),
                                    start=False, stop=t.last, skip_group_check=True)
                ins.then_inc(tile_used, 1)

            def turn(g):
                pe.wait_ge(norm_done, g + 1)
                if g:
                    pe.wait_ge(u_done, g)
                if g == A_GROUPS:
                    pe.wait_ge(p_done, 1)
                for k in range(GROUP):
                    ins = pe.transpose(ps_t[:, k * P:(k + 1) * P], x1n[:, k, :], ident)
                ins.then_inc(t_done, 1)

            def project(g):
                pe.wait_ge(t_copied, g + 1)
                if g:
                    pe.wait_ge(v_done, g)
                for k in range(GROUP):
                    pe.matmul(ps_h[:, k * P:(k + 1) * P], x1T[:, k * P:(k + 1) * P], w1_sb,
                              start=True, stop=True)
                for k in range(GROUP):
                    ins = pe.matmul(ps_t[:, k:k + 1], x1T[:, k * P:(k + 1) * P], wf[:, :], start=True, stop=True)
                ins.then_inc(h_done, 1)

            stages = {"turn": turn, "project": project}

            for jt in range(RING):
                if jt:
                    for c in [[4, 5], [6], [7]][jt - 1]:
                        el_rows(c)
                tile0(Tile(0, jt))
            turns(pe, 0, RING, TURNS - 2, tile0)
            for jt in range(TILES - RING, TILES):
                tile0(Tile(0, jt))
            for jt in range(TILES):
                for stage, g in plan0["pe"].get(jt, []):
                    stages[stage](g)
                if jt == 28:
                    pe.wait_ge(k_part, 1)
                    pe.matmul(ps_t[0:1, 0:P], kpart[:, :], ident, start=True, stop=True).then_inc(k_row, 1)
                if jt == 30:
                    pe.wait_ge(k_one, 1)
                    pe.matmul(ps_t[:, 256:257], ones[0:1, 0:P], k1[:, :], start=True, stop=True)\
                      .then_inc(k_bcast, 1)
                tile0(Tile(1, jt))

            def tile1(t):
                pe.wait_ge(scaled_a if t.resident else scaled_v, (t.w - L1) * RESIDENT + t.half + 1)
                v = V_v[:, bass.ds(t.jt, 1), :].rearrange("p a c -> p (a c)")
                for n in range(BLOCKS[t.w]):
                    bank = BANK0[t.w] + n // PER_BANK
                    if t.first and n % PER_BANK == 0:
                        bank_ready(t.w, bank)
                        clear(bank)
                    for part in range(2):
                        ins = pe.matmul(acc_of(n, BANK0[t.w]), pair16[:, t.slot, n * P:(n + 1) * P],
                                        v[:, part * DV:part * DV + DA], start=False,
                                        stop=t.last, skip_group_check=True)
                ins.then_inc(tile_used, 1)

            pe.wait_ge(v_done, A_GROUPS)
            for jt in range(HB):
                for stage, g in plan1["pe"].get(jt, []):
                    stages[stage](g)
                tile1(Tile(L1, jt))
            turns(pe, L1, HB, A_GROUPS - 1, tile1, lambda i: pe.wait_ge(v_done, i + A_GROUPS + 1))
            pe.wait_ge(v_done, GROUPS)
            pe.wait_ge(mean_in, 2)
            pe.matmul(ps_t[:, 0:P], xmb[:, :], w1_sb, start=True, stop=True).then_inc(mean_mm, 1)
            for jt in range(TILES - RING, TILES):
                tile1(Tile(L1, jt))
            for w in (L1 + 1, L1 + 2):
                for jt in range(RING):
                    tile1(Tile(w, jt))
                turns(pe, w, RING, TURNS - 2, tile1)
                for jt in range(TILES - RING, TILES):
                    tile1(Tile(w, jt))
            pe.wait_ge(far_done, 1)
            pe.matmul(ps_t[0:1, 256:257], far_any[:, :], ones[:, 0:1], start=True, stop=True).then_inc(far_sum, 1)
            pe.wait_ge(flag_done, 2)
            far_nodes = pe.value_load(flag[0:1, 0:1], min_val=0, max_val=N)
            with pe.If(far_nodes > 0):
                pe.wait_ge(g_w, 1)
                with pe.Fori(0, GROUPS) as g:
                    pe.wait_ge(g_x, g + 1)
                    for k in range(GROUP):
                        ins = pe.transpose(ps_t[:, k * P:(k + 1) * P], x1n[:, k, :], ident)
                    ins.then_inc(g_t, 1)
                    pe.wait_ge(g_tc, g + 1)
                    pe.matmul(acc[:, 0, :], wfb[:, :], x1T[:, :], start=True, stop=True).then_inc(g_f, 1)
                    for k in range(GROUP):
                        ins = pe.matmul(acc[:, 1, k * P:(k + 1) * P], x1T[:, k * P:(k + 1) * P], w1_sb,
                                        start=True, stop=True)
                    ins.then_inc(g_h, 1)
                with pe.Fori(0, TILES) as t:
                    pe.wait_ge(g_exp, t + 1)
                    for c in range(GROUPS + 1):
                        if c < GROUPS:
                            if c >= 2:
                                pe.wait_ge(g_tcopy, t * GROUPS + c - 1)
                            for k in range(GROUP):
                                ins = pe.transpose(small[c % 2][:, k * P:(k + 1) * P],
                                                   e_row[:, (c * GROUP + k) * P:(c * GROUP + k + 1) * P], ident)
                            ins.then_inc(g_turn, 1)
                        if c:
                            pe.wait_ge(g_tcopy, t * GROUPS + c)
                            for k in range(GROUP):
                                jt = (c - 1) * GROUP + k
                                ins = pe.matmul(acc[:, 0, 0:D],
                                                t_row[:, (c - 1) % 2 * BANK + k * P:(c - 1) % 2 * BANK + (k + 1) * P],
                                                hfull[:, jt, :], start=jt == 0, stop=jt == TILES - 1)
                            if c == GROUPS:
                                ins.then_inc(g_acc, 1)


def kernel(x, adj, L0_gnn_weight, L0_gnn_a_l, L0_gnn_a_r, L0_gnn_b, L1_gnn_w, L1_gnn_w_a, L1_gnn_a):
    import concourse.bacc as bacc
    from concourse.bass_utils import run_bass_kernel_spmd

    x, adj = np.asarray(x), np.asarray(adj)
    W, w = np.asarray(L0_gnn_weight), np.asarray(L1_gnn_w)
    weights = np.zeros((P, W_COLS), np.float32)
    b = np.broadcast_to(np.asarray(L0_gnn_b), (P, D))
    a_lr = np.stack([np.asarray(L0_gnn_a_l), np.asarray(L0_gnn_a_r)], axis=1)
    parts = [W, W.T, w, w.T, b, np.eye(P, dtype=np.float32), a_lr,
             np.asarray(L1_gnn_w_a).T, np.asarray(L1_gnn_a)[2:4]]
    for part, at in zip(parts, W_AT):
        weights[:part.shape[0], at:at + part.shape[1]] = part
    arrays = {
        "adjT": adj.T.reshape(TILES, P, 2, HALF).transpose(2, 0, 1, 3),
        "adj": adj, "xT": x.T, "x": x, "weights": weights,
    }
    arrays = {"in_" + k: np.ascontiguousarray(v) for k, v in arrays.items()}
    nc = bacc.Bacc("TRN2", target_bir_lowering=False, num_devices=1)
    args = [nc.dram_tensor(k, v.shape, mybir.dt.from_np(v.dtype), kind="ExternalInput").ap()
            for k, v in arrays.items()]
    out = nc.dram_tensor("rows_out", (N, D), F32, kind="ExternalOutput").ap()
    build(nc, *args, out)
    r = run_bass_kernel_spmd(nc, [arrays], core_ids=[0])
    return r.results[0]["rows_out"]
```

```python
from contextlib import ExitStack

import numpy as np

import concourse.bass as bass
from concourse import mybir

ALU = mybir.AluOpType
ACT = mybir.ActivationFunctionType
F32 = mybir.dt.float32
F16 = mybir.dt.float16
BF16 = mybir.dt.bfloat16
I8 = mybir.dt.int8
I32 = mybir.dt.int32
AX = mybir.AxisListType

P = 128
N = 4096
D = 128
DA = D + 1
DV = D + 2
TILES = N // P
HALF = N // 2
HB = HALF // P
QB = HB // 2
RING = 4
STEP = 2 * RING
TURNS = TILES // RING
AHEAD = 2
BANK = 512
PER_BANK = BANK // DA
BANKS = -(-HB // PER_BANK)
SLOTS = BANKS * PER_BANK
H_GROUPS = -(-TILES // 3)
START = H_GROUPS + 1
GROUP = 4
GROUPS = TILES // GROUP
FIN = 4
A_GROUPS = GROUPS // 2
RESIDENT = TILES // 2
SWEEPS0 = 2
L1 = 2
SLOPE = 0.2
EPS = 1e-5
TINY = 1e-12
LOG2E = 1.4426950408889634
LN2_HI = 355.0 / 512.0
LN2_LO = -2.12194440e-4
EXPONENT = 1 << 23
EXP_MASK = 0x7F800000
V_SCALE = 13
W_WIDTHS = [D + 2, D, D, D, D, P, 2, P, 1]
W_AT = [sum(W_WIDTHS[:k]) for k in range(len(W_WIDTHS) + 1)]
W_COLS = W_AT[-1]
NEG_INF = -1e18
TE_LOW, TE_HIGH = 47.0, 187.0


class Chain:

    def __init__(self, eng, sem, call, per):
        self.eng, self.sem, self.call, self.per, self.k = eng, sem, call, per, 0

    def inc(self, ins):
        self.k += 1
        ins.then_inc(self.sem, 1)

    def wait(self):
        self.eng.wait_ge(self.sem, self.call * self.per + self.k)

    def step(self, ins):
        self.inc(ins)
        self.wait()

    def end(self):
        assert self.k == self.per, (self.k, self.per)


class Tile:

    def __init__(self, w, base, i=0, step=0):
        self.w, self.base = w, base
        self.fixed = step == 0
        self.jt = base + i * step
        self.n = w * TILES + self.jt
        self.slot = base % RING
        self.turn = w * TURNS + base // RING + i * (step // RING)
        self.resident = base % 2 == 0
        self.half = base // 2 + i * (step // 2)
        self.again_slot = base // 2 % 2
        self.first = self.fixed and base == 0
        self.last = self.fixed and base == TILES - 1
        self.at = (i, step)

    def ahead(self, k):
        if self.fixed and self.base + k >= TILES:
            return Tile(self.w + 1, self.base + k - TILES)
        return Tile(self.w, self.base + k, *self.at)


def turns(eng, w, lo, hi, tile, step=RING, before=None):
    with eng.Fori(0, (hi - lo) // step) as i:
        for u in range(step):
            if before and u % RING == 0:
                before(i * (step // RING) + u // RING)
            tile(Tile(w, lo + u, i, step))


def build(nc, adjT, adj, xT, x, weights_d, out):
    with ExitStack() as ctx:
        def sb(name, shape, dt=F32):
            return ctx.enter_context(nc.sbuf_tensor(name, shape, dt))

        def sem(name):
            return ctx.enter_context(nc.semaphore(name))

        signs = sb("signs", [P, RESIDENT, N], I8)
        adj_ring = sb("adj_ring", [P, RING, HALF])
        pair = sb("pair", [P, RING, HALF])
        pair16 = pair[:, :, :].bitcast(BF16)
        V = sb("V", [P, TILES * 2 * DV], F16)
        V_v = V[:, :].rearrange("p (t c) -> p t c", c=2 * DV)
        elb = [V[:, h * HB * 2 * DV:h * HB * 2 * DV + 2 * HALF].bitcast(F32) for h in range(2)]
        haug = sb("haug", [P, TILES, DA])
        obuf = haug[:, 0:HB, 0:D]
        fin = haug[:, HB:2 * HB, 0:D]
        xs = sb("xs", [P, TILES, D])
        read0 = sb("read0", [P, HB - BANKS // 2 * PER_BANK, D])
        xT_sb = signs[:, RESIDENT - 4:RESIDENT, :].rearrange("p t n -> p (t n)").bitcast(F32)
        weights = sb("weights", [P, W_COLS])
        w0, w0T, w1_sb, w1T_sb, bb, ident, alr, waT_f, adst_f = (
            weights[:, a:z] for a, z in zip(W_AT, W_AT[1:]))
        waT, adst = waT_f[0:2, :], adst_f[0:2, :]
        wad = sb("wad", [P, 1])
        wf = sb("wf", [P, 1])
        ones = sb("ones", [P, D])
        walb = sb("walb", [P, P])
        xmb = sb("xmb", [P, P])
        zeros = sb("zeros", [P, PER_BANK * DA], BF16)
        elr = sb("elr", [P, TILES, 2])
        Fj = sb("Fj", [P, TILES])
        fe = sb("fe", [P, 2, SLOTS])
        den = sb("den", [P, SLOTS])
        coef = sb("coef", [P, SLOTS])
        none = sb("none", [P, SLOTS])
        stats = sb("stats", [P, GROUP, 6])
        scratch = sb("scratch", [P, 2])
        mv = [sb(f"mv{k}", [P, GROUP, 2]) for k in range(2)]
        veps = [sb(f"veps{k}", [P, GROUP]) for k in range(2)]
        rstd = [sb(f"rstd{k}", [P, GROUP]) for k in range(2)]
        shift = [sb(f"shift{k}", [P, GROUP]) for k in range(2)]
        half_neg = sb("half_neg", [P, GROUP])
        x1n = sb("x1n", [P, GROUP, D])
        x1T = sb("x1T", [P, GROUP * P])
        xsum = sb("xsum", [P, GROUPS])
        xtot = sb("xtot", [P, 1])
        hmean = sb("hmean", [P, D])
        k_int = sb("k_int", [P, GROUP], I32)
        u1 = sb("u1", [P, GROUP])
        u2 = sb("u2", [P, GROUP])
        rj = sb("rj", [P, GROUP])
        hmax = sb("hmax", [P, GROUP])
        hmax1 = sb("hmax1", [P, GROUP])
        hexp = sb("hexp", [P, GROUP], I32)
        hinv = sb("hinv", [P, GROUP], I32)
        q = sb("q", [P, GROUP])
        kf = sb("kf", [P, TILES])
        hef = sb("hef", [P, TILES])
        te = sb("te", [P, TILES])
        tec = sb("tec", [P, TILES])
        pj = sb("pj", [P, TILES], I32)
        pj_f = pj[:, :].bitcast(F32)
        kpart = sb("kpart", [P, 1])
        k1 = sb("k1", [1, 1])
        Kb = sb("Kb", [P, 1])
        far = sb("far", [P, 2, TILES])
        far_any = sb("far_any", [P, 1])
        flag = sb("flag", [1, 1], I32)
        fb = V[:, 0:2 * N].bitcast(F32)
        hfull = haug[:, :, 0:D]
        adj_row = adj_ring[:, 0:2, :].rearrange("p a n -> p (a n)")
        e_row = pair[:, 0:2, :].rearrange("p a n -> p (a n)")
        t_row = pair[:, 2:4, :].rearrange("p a n -> p (a n)")
        wfb = sb("wfb", [P, P])
        g_max = sb("g_max", [P, 1])
        g_sum = sb("g_sum", [P, 1])
        g_rec = sb("g_rec", [P, 1])
        g_y = sb("g_y", [P, D])
        g_out = sb("g_out", [P, D])

        acc = ctx.enter_context(nc.psum_tensor("acc", [P, BANKS, BANK], F32))
        ps_t = ctx.enter_context(nc.psum_tensor("ps_t", [P, BANK], F32))
        ps_h = ctx.enter_context(nc.psum_tensor("ps_h", [P, BANK], F32))
        small = [ps_t, ps_h]

        def el_bank(c):
            return acc[:, c % BANKS, :]

        def acc_of(block, bank0=0):
            c = block % PER_BANK * DA
            return acc[:, bank0 + block // PER_BANK, c:c + DA]

        def den_of(bank0, lo, hi):
            return acc[:, bank0 + lo:bank0 + hi, 0:PER_BANK * DA].rearrange(
                "p k (s c) -> p k s c", c=DA)[:, :, :, D]

        def by_bank(t, lo, hi):
            return t[:, lo * PER_BANK:hi * PER_BANK].rearrange("p (k s) -> p k s", s=PER_BANK)

        w_in = sem("w_in")
        xT_in = [sem(f"xT_in{c}") for c in range(4)]
        x_in = sem("x_in")
        consts = sem("consts")
        wa_done = sem("wa_done")
        wa_copied = sem("wa_copied")
        el_done = sem("el_done")
        el_copied = sem("el_copied")
        h0_done = sem("h0_done")
        elr_copied = sem("elr_copied")
        F_done = sem("F_done")
        haug_done = sem("haug_done")
        fe_done = sem("fe_done")
        xb_done = sem("xb_done")
        adj_in = [sem(f"adj_in{s}") for s in range(RING)]
        again_in = [sem(f"again_in{s}") for s in range(2)]
        scored_v = sem("scored_v")
        scored_a = sem("scored_a")
        exped = sem("exped")
        masked = sem("masked")
        scaled_v = sem("scaled_v")
        scaled_a = sem("scaled_a")
        tile_used = sem("tile_used")
        first_done = sem("first_done")
        coef_done = sem("coef_done")
        freed_v = sem("freed_v")
        freed_a = sem("freed_a")
        y0_added = sem("y0_added")
        own = {k: sem(f"own_{k}") for k in ("y", "var", "pow", "parts", "mask", "coef", "stats", "tail", "mean", "k", "far")}
        var_done = sem("var_done")
        rstd_done = sem("rstd_done")
        norm_done = sem("norm_done")
        x1_kept = sem("x1_kept")
        t_done = sem("t_done")
        t_copied = sem("t_copied")
        h_done = sem("h_done")
        u_done = sem("u_done")
        r_done = sem("r_done")
        q_done = sem("q_done")
        hi_done = sem("hi_done")
        v_done = sem("v_done")
        k_part = sem("k_part")
        k_row = sem("k_row")
        k_one = sem("k_one")
        k_bcast = sem("k_bcast")
        p_done = sem("p_done")
        mean_in = sem("mean_in")
        mean_mm = sem("mean_mm")
        mean_done = sem("mean_done")
        x1_added = sem("x1_added")
        stats_done = sem("stats_done")
        y_done = sem("y_done")
        shift_done = sem("shift_done")
        last_done = sem("last_done")
        stored = [sem(f"stored{s}") for s in range(FIN)]
        far_done = sem("far_done")
        far_sum = sem("far_sum")
        flag_done = sem("flag_done")
        g_w = sem("g_w")
        g_x = sem("g_x")
        g_t = sem("g_t")
        g_tc = sem("g_tc")
        g_f = sem("g_f")
        g_fc = sem("g_fc")
        g_h = sem("g_h")
        g_hc = sem("g_hc")
        g_adj = sem("g_adj")
        g_own = sem("g_own")
        g_e = sem("g_e")
        g_exp = sem("g_exp")
        g_turn = sem("g_turn")
        g_tcopy = sem("g_tcopy")
        g_acc = sem("g_acc")
        g_var = sem("g_var")
        g_pow = sem("g_pow")
        g_row = sem("g_row")
        g_stored = sem("g_stored")

        BLOCKS = [HB, HB, HB, QB, QB]
        COL0 = [0, HALF, 0, HALF, HALF + QB * P]
        BANK0 = [0, 0, 0, 0, BANKS // 2]
        NBANKS = [-(-n // PER_BANK) for n in BLOCKS]
        FIRST = [BANKS // 2, BANKS // 2, BANKS // 2, 1, 1]
        DVE_BANKS = [[0, 1, 2], [0, 1, 2], [0, 2, 4], [0], [0]]
        ACT_BANKS = [[k for k in range(n) if k not in d] for n, d in zip(NBANKS, DVE_BANKS)]
        SHARE = len(DVE_BANKS[0]) * PER_BANK

        def read_before(banks, w, bank=None):
            return sum(len(banks[v]) for v in range(w)) + (banks[w].index(bank) + 1 if bank is not None else 0)

        def blocks_of(w, bank):
            return range(bank * PER_BANK, min((bank + 1) * PER_BANK, BLOCKS[w]))

        def obuf_row(w, n):
            return n + (QB if w == L1 + 2 else 0)
        def tiles_used(eng, t):
            if t.w or t.base >= RING:
                eng.wait_ge(tile_used, t.n - RING + 1)

        def slot_free1(eng, t):
            if t.w == L1 and t.base < RING:
                eng.wait_ge(masked, t.n - RING + 1)
            else:
                eng.wait_ge(tile_used, t.n - RING + 1)

        def adj_arrived(eng, t):
            eng.wait_ge(adj_in[t.slot], 16 * (t.turn + 1))

        def scores_by_act(t):
            return t.slot == RING - 1

        def cols_of(w):
            return slice(COL0[w], COL0[w] + BLOCKS[w] * P)

        plan0 = {e: {} for e in ("pe", "act", "dve")}
        plan1 = {e: {} for e in ("pe", "act", "dve")}

        def at(plan, tile, stage, g):
            plan.setdefault(tile, []).append((stage, g))

        for k in range(A_GROUPS):
            b0 = 1 + 6 * k
            at(plan0["dve"], b0, "variance", k)
            at(plan0["pe"], b0 + 2, "turn", k)
            at(plan0["act"], b0 + 5, "copy_T", k)
            at(plan0["pe"], b0 + 4, "project", k)
            at(plan0["dve"], b0 + 6, "powers", k)
            at(plan0["act"], b0 + 8, "exp_r", k)
            at(plan0["dve"], b0 + 8, "parts", k)
            at(plan0["act"], b0 + 10, "high", k)
            at(plan0["dve"], b0 + 10, "low", k)
            b1, g = 5 * k, A_GROUPS + k
            at(plan1["dve"], b1, "variance", g)
            at(plan1["dve"], b1 + 1, "norm", g)
            at(plan1["pe"], b1 + 2, "turn", g)
            at(plan1["act"], b1 + 4, "copy_T", g)
            at(plan1["pe"], b1 + 4, "project", g)
            at(plan1["dve"], b1 + 6, "powers", g)
            at(plan1["act"], b1 + 7, "exp_r", g)
            at(plan1["dve"], b1 + 7, "parts", g)
            at(plan1["act"], b1 + 8, "high", g)
            at(plan1["dve"], b1 + 8, "low", g)
        plan2 = {e: {} for e in ("act", "dve")}
        for k in range(3):
            b2 = 5 + 8 * k
            at(plan2["dve"], b2, "last_y", k)
            at(plan2["dve"], b2 + 2, "last_var", k)
            at(plan2["dve"], b2 + 4, "last_shift", k)
            at(plan2["act"], b2 + 7, "finish", k)
        for p in (plan0["dve"], plan1["dve"], plan2["dve"]):
            for tile in p:
                p[tile].sort(key=lambda s: s[1])

        def rows_out(g):
            return (out.rearrange("(t p) d -> p t d", p=P)[:, g * GROUP:(g + 1) * GROUP, :],
                    fin[:, g % FIN * GROUP:(g % FIN + 1) * GROUP, :])

        def last_rows(g):
            if g < HB // GROUP:
                return obuf[:, g * GROUP:(g + 1) * GROUP, :], g * GROUP
            g -= HB // GROUP
            return obuf[:, g * GROUP:(g + 1) * GROUP, :], g % (QB // GROUP) * GROUP

        block = ctx.enter_context(nc.Block())

        @block.sync
        def _(sp):
            def load_xT(c):
                sp.dma_start(xT_sb[:, c * 1024:(c + 1) * 1024],
                             xT[:, c * 1024:(c + 1) * 1024]).then_inc(xT_in[c], 16)

            def load(t):
                tiles_used(sp, t)
                sp.dma_start(adj_ring[:, t.slot, :],
                             adjT[t.w, bass.ds(t.jt, 1), :, :].rearrange("a p n -> p (a n)"))\
                  .then_inc(adj_in[t.slot], 16)

            sp.dma_start(weights[:, :], weights_d).then_inc(w_in, 16)
            load_xT(0)
            load_xT(1)
            load(Tile(0, 0))
            load_xT(2)
            load_xT(3)
            for jt in range(1, RING):
                load(Tile(0, jt))
            sp.dma_start(xs[:, :, :], x.rearrange("(t p) d -> p t d", p=P)).then_inc(x_in, 16)
            turns(sp, 0, RING, TILES, load)
            turns(sp, 1, 0, TILES, load)

            def load_again(t):
                if t.w == L1 and t.base < RING:
                    sp.wait_ge(tile_used, L1 * TILES - RING + t.again_slot + 1)
                else:
                    sp.wait_ge(scaled_v, (t.w - L1) * RESIDENT + t.half - 1)
                off = COL0[t.w] % HALF
                cols = BLOCKS[t.w] * P
                sp.dma_start(adj_ring[:, t.again_slot, 0:cols],
                             adjT[COL0[t.w] // HALF, bass.ds(t.jt, 1), :, off:off + cols]
                             .rearrange("a p n -> p (a n)")).then_inc(again_in[t.again_slot], 16)

            def odd(t):
                if not t.resident:
                    load_again(t)

            for jt in range(RING):
                odd(Tile(L1, jt))
            turns(sp, L1, RING, TILES, odd)
            turns(sp, L1 + 1, 0, TILES, odd)
            turns(sp, L1 + 2, 0, TILES, odd)
            sp.wait_ge(last_done, 1)
            sp.dma_start(*rows_out(GROUPS - 1)).then_inc(stored[(GROUPS - 1) % FIN], 16)
            for s in range(FIN):
                sp.wait_ge(stored[s], 16 * (GROUPS // FIN))
            sp.wait_ge(flag_done, 2)
            far_nodes = sp.value_load(flag[0:1, 0:1], min_val=0, max_val=N)
            with sp.If(far_nodes > 0):
                with sp.Fori(0, TILES) as t:
                    sp.wait_ge(g_e, t * 3 + 2)
                    sp.dma_start(adj_row, adj.rearrange("(t p) n -> t p n", p=P)[bass.ds(t, 1), :, :]
                                 .rearrange("a p n -> p (a n)")).then_inc(g_adj, 16)
                    sp.wait_ge(g_row, t + 1)
                    sp.dma_start(out.rearrange("(t p) d -> t p d", p=P)[bass.ds(t, 1), :, :]
                                 .rearrange("a p d -> p (a d)"), g_out[:, :]).then_inc(g_stored, 16)

        @block.gpsimd
        def _(pool):
            pool.memset(ones[:, :], 1.0).then_inc(consts, 1)
            pool.memset(zeros[:, :], 0.0).then_inc(consts, 1)
            pool.memset(fe[:, :, :], 1.0).then_inc(consts, 1)
            pool.memset(half_neg[:, :], -0.5).then_inc(consts, 1)
            pool.wait_ge(x_in, 16)
            pool.wait_ge(w_in, 16)
            pool.tensor_tensor(xs[:, :, :], xs[:, :, :],
                               bb.unsqueeze(1).to_broadcast([P, TILES, D]), ALU.add).then_inc(xb_done, 1)
            pool.wait_ge(consts, 4)
            pool.wait_ge(xb_done, 1)

            def add_share(w):
                pool.wait_ge(freed_a, read_before(ACT_BANKS, w + 1))
                ys = xs[:, w * HB + SHARE:(w + 1) * HB, :]
                pool.tensor_tensor(ys, ys, read0[:, 0:HB - SHARE, :], ALU.add).then_inc(y0_added, 1)

            def rsqrt(c, k=0):
                c.step(pool.tensor_tensor(rstd[k][:, :], veps[k][:, :], half_neg[:, :], ALU.pow))

            def keep(g):
                pool.wait_ge(norm_done, g + 1)
                pool.tensor_copy(xs[:, g * GROUP:(g + 1) * GROUP, :], x1n[:, :, :]).then_inc(x1_kept, 1)

            add_share(0)
            for g in range(GROUPS):
                if g == A_GROUPS:
                    add_share(1)
                pool.wait_ge(var_done, g + 1)
                rsqrt(Chain(pool, rstd_done, g, 1))
                if g < A_GROUPS:
                    if g:
                        pool.wait_ge(t_done, g)
                        pool.wait_ge(x1_kept, g)
                    for k in range(GROUP):
                        ins = pool.tensor_scalar(x1n[:, k, :], xs[:, g * GROUP + k, :], mv[0][:, k, 0:1],
                                                 rstd[0][:, k:k + 1], ALU.subtract, ALU.mult)
                    ins.then_inc(norm_done, 1)
                keep(g)

            def add_x1(g):
                w = L1 + (g >= HB // GROUP)
                pool.wait_ge(freed_v, read_before(DVE_BANKS, w + 1))
                pool.wait_ge(freed_a, read_before(ACT_BANKS, w + 1))
                rows = last_rows(g)[0]
                pool.tensor_tensor(rows, rows, xs[:, g * GROUP:(g + 1) * GROUP, :], ALU.add)\
                    .then_inc(x1_added, 1)

            def last_rsqrt(g):
                pool.wait_ge(y_done, g + 1)
                rsqrt(Chain(pool, rstd_done, GROUPS + g, 1), g % 2)

            add_x1(0)
            for g in range(4):
                if g < 3:
                    add_x1(g + 1)
                last_rsqrt(g)
            add_x1(4)
            add_x1(5)
            for g in range(4, GROUPS):
                last_rsqrt(g)
            pool.wait_ge(flag_done, 2)
            far_nodes = pool.value_load(flag[0:1, 0:1], min_val=0, max_val=N)
            with pool.If(far_nodes > 0):
                with pool.Fori(0, TILES) as t:
                    pool.wait_ge(g_var, t + 1)
                    pool.tensor_tensor(rstd[0][:, :], veps[0][:, :], half_neg[:, :], ALU.pow).then_inc(g_pow, 1)

        @block.scalar
        def _(act):
            def copy_el(c):
                act.wait_ge(el_done, c + 1)
                act.activation(elb[c // 4][:, c % 4 * BANK:(c % 4 + 1) * BANK], el_bank(c), ACT.Copy)\
                   .then_inc(el_copied, 1)

            def exp_F(a):
                t0 = 3 * a
                n = min(3, TILES - t0)
                act.wait_ge(elr_copied, a + 1)
                act.activation(Fj[:, t0:t0 + n], elr[:, t0:t0 + n, 1], ACT.Exp, scale=SLOPE).then_inc(F_done, 1)

            def tile0(t):
                s = t.slot
                if scores_by_act(t):
                    if t.w or t.base >= RING:
                        act.wait_ge(masked, t.n - RING + 1)
                    act.activation(pair[:, s, :], elb[t.w], ACT.Relu, bias=elr[:, bass.ds(t.jt, 1), 1])\
                       .then_inc(scored_a, 1)
                    act.wait_ge(scored_a, t.turn + 1)
                else:
                    act.wait_ge(scored_v, t.turn * (RING - 1) + s + 1)
                ins = act.activation(pair[:, s, :], pair[:, s, :], ACT.Exp, scale=1.0 - SLOPE)
                if t.resident:
                    adj_arrived(act, t)
                    ins = act.activation(signs[:, bass.ds(t.half, 1), COL0[t.w]:COL0[t.w] + HALF]
                                         .rearrange("p a n -> p (a n)"), adj_ring[:, s, :], ACT.Sign)
                ins.then_inc(exped, 1)

            def read_out(w, parts=(0, 1)):
                if w == 1:
                    act.wait_ge(y0_added, 1)
                if w > L1:
                    act.wait_ge(norm_done, GROUPS + (2 if w == L1 + 1 else 4))
                for bank in ACT_BANKS[w]:
                    if (bank >= FIRST[w]) not in parts:
                        continue
                    act.wait_ge(coef_done, 2 * w + 1 + (bank >= FIRST[w]))
                    for n in blocks_of(w, bank):
                        dst = read0[:, n - SHARE, :] if w < L1 else obuf[:, obuf_row(w, n), :]
                        ins = act.activation(dst, acc_of(n, BANK0[w])[:, 0:D],
                                             ACT.Relu if w >= L1 else ACT.Copy, scale=coef[:, n:n + 1])
                    ins.then_inc(freed_a, 1)

            def copy_T(g):
                act.wait_ge(t_done, g + 1)
                if g:
                    act.wait_ge(h_done, g)
                act.activation(x1T[:, :], ps_t[:, :], ACT.Identity,
                               accum_out=xsum[:, g:g + 1]).then_inc(t_copied, 1)

            def exp_r(g):
                act.wait_ge(u_done, g + 1)
                act.activation(rj[:, :], u2[:, :], ACT.Exp).then_inc(r_done, 1)

            def high(g):
                act.wait_ge(q_done, g + 1)
                for k in range(GROUP):
                    ins = act.activation(V_v[:, g * GROUP + k, 0:D], ps_h[:, k * P:(k + 1) * P],
                                         ACT.Copy, scale=q[:, k:k + 1])
                ins.then_inc(hi_done, 1)

            stages = {"copy_T": copy_T, "exp_r": exp_r, "high": high}

            def scale(t):
                if not t.resident:
                    return
                slot_free1(act, t)
                act.activation(pair16[:, t.slot, 0:BLOCKS[t.w] * P],
                               signs[:, bass.ds(t.half, 1), cols_of(t.w)].rearrange("p a n -> p (a n)"),
                               ACT.Relu, scale=pj_f[:, bass.ds(t.jt, 1)]).then_inc(scaled_a, 1)

            for c in range(4):
                copy_el(c)
            exp_F(0)
            for jt in range(START):
                tile0(Tile(0, jt))
                if jt == 0:
                    for c in range(4, 8):
                        copy_el(c)
                    exp_F(1)
                if 2 <= jt - 2 < H_GROUPS:
                    exp_F(jt - 2)
            exp_F(H_GROUPS - 1)
            turns(act, 0, START, TILES - RING, tile0, STEP)
            for jt in range(TILES - RING, TILES):
                tile0(Tile(0, jt))
            for h in range(2):
                act.activation(fe[:, h, 0:HB], elr[:, h * HB:(h + 1) * HB, 0], ACT.Exp, scale=SLOPE)\
                   .then_inc(fe_done, 1)
            for jt in range(TILES):
                if jt == 2:
                    read_out(0)
                for stage, g in plan0["act"].get(jt, []):
                    stages[stage](g)
                tile0(Tile(1, jt))

            act.wait_ge(p_done, 1)
            for jt in range(TILES):
                if jt == 3:
                    read_out(1)
                for stage, g in plan1["act"].get(jt, []):
                    stages[stage](g)
                if jt >= HB and jt % GROUP == 0:
                    act.wait_ge(p_done, (jt - HB) // GROUP + 2)
                scale(Tile(L1, jt))

            def finish(g):
                k = g % 2
                rows = last_rows(g)[0]
                act.wait_ge(shift_done, g + 1)
                if g >= FIN:
                    act.wait_ge(stored[g % FIN], 16 * (g // FIN))
                for n in range(GROUP):
                    ins = act.activation(fin[:, g % FIN * GROUP + n, :], rows[:, n, :], ACT.Identity,
                                         bias=shift[k][:, n:n + 1], scale=rstd[k][:, n:n + 1])
                ins.then_inc(norm_done, 1)
                act.wait_ge(norm_done, GROUPS + g + 1)
                act.dma_start(*rows_out(g)).then_inc(stored[g % FIN], 16)

            for w in (L1 + 1, L1 + 2):
                scale(Tile(w, 0))
                if w == L1 + 1:
                    read_out(w - 1, (0,))
                scale(Tile(w, 2))
                read_out(w - 1, (1,) if w == L1 + 1 else (0, 1))
                for jt in range(RING, TILES):
                    for stage, k in plan2["act"].get(jt, []):
                        finish(k + (w - L1 - 1) * 3)
                    scale(Tile(w, jt))
            read_out(L1 + 2)
            finish(GROUPS - 2)
            act.wait_ge(flag_done, 2)
            far_nodes = act.value_load(flag[0:1, 0:1], min_val=0, max_val=N)
            with act.If(far_nodes > 0):
                with act.Fori(0, GROUPS) as g:
                    act.wait_ge(g_t, g + 1)
                    act.activation(x1T[:, :], ps_t[:, :], ACT.Copy).then_inc(g_tc, 1)
                    act.wait_ge(g_f, g + 1)
                    act.activation(fb[:, bass.ds(g * BANK, BANK)], acc[:, 0, :], ACT.Copy).then_inc(g_fc, 1)
                    act.wait_ge(g_h, g + 1)
                    act.activation(hfull[:, bass.ds(g * GROUP, GROUP), :],
                                   acc[:, 1, :].rearrange("p (k d) -> p k d", d=D), ACT.Copy).then_inc(g_hc, 1)
                with act.Fori(0, TILES) as t:
                    act.wait_ge(g_e, t * 3 + 5)
                    act.activation(e_row, e_row, ACT.Exp, bias=g_max[:, 0:1], accum_out=g_sum[:, 0:1])\
                       .then_inc(g_exp, 1)
                    for c in range(GROUPS):
                        act.wait_ge(g_turn, t * GROUPS + c + 1)
                        act.activation(t_row[:, c % 2 * BANK:(c % 2 + 1) * BANK], small[c % 2][:, :], ACT.Copy)\
                           .then_inc(g_tcopy, 1)

        @block.vector
        def _(dve):
            dve.wait_ge(wa_done, 1)
            dve.tensor_copy(w0[:, D:D + 2], ps_t[:, 0:2]).then_inc(wa_copied, 1)
            dve.tensor_copy(wad[:, :], ps_t[:, 8:9]).then_inc(wa_copied, 1)
            dve.wait_ge(wa_copied, 2)
            dve.wait_ge(consts, 3)
            dve.tensor_scalar(walb[:, :], ones[:, :], w0[:, D:D + 1], None, ALU.mult).then_inc(wa_copied, 1)
            dve.wait_ge(wa_done, 2)
            dve.tensor_copy(wf[:, :], ps_t[:, 16:17]).then_inc(wa_copied, 1)

            def copy_elr(a):
                t0 = 3 * a
                n = min(3, TILES - t0)
                ps = small[a % 2][:, 0:n * (D + 2)].rearrange("p (t c) -> p t c", c=D + 2)
                dve.wait_ge(h0_done, a + 1)
                dve.tensor_copy(elr[:, t0:t0 + n, :], ps[:, :, D:D + 2]).then_inc(elr_copied, 1)

            def weigh_h(a):
                t0 = 3 * a
                n = min(3, TILES - t0)
                ps = small[a % 2][:, 0:n * (D + 2)].rearrange("p (t c) -> p t c", c=D + 2)
                dve.wait_ge(F_done, a + 1)
                dve.tensor_tensor(haug[:, t0:t0 + n, 0:D], ps[:, :, 0:D],
                                  Fj[:, t0:t0 + n].unsqueeze(2).to_broadcast([P, n, D]), ALU.mult)
                dve.tensor_copy(haug[:, t0:t0 + n, D], Fj[:, t0:t0 + n]).then_inc(haug_done, 1)

            def score(t):
                if scores_by_act(t) or t.w == L1:
                    return
                if t.w or t.base >= RING:
                    dve.wait_ge(masked, t.n - RING + 1)
                dve.tensor_scalar(pair[:, t.slot, :], elb[t.w], elr[:, bass.ds(t.jt, 1), 1], 0.0,
                                  ALU.add, ALU.max).then_inc(scored_v, 1)

            def mask(t):
                s = t.slot
                dve.wait_ge(exped, t.n + 1)
                adj_arrived(dve, t)
                dve.scalar_tensor_tensor(out=adj_ring[:, s, :], in0=adj_ring[:, s, :], scalar=0.0,
                                         in1=pair[:, s, :], op0=ALU.not_equal, op1=ALU.mult)\
                   .then_inc(masked, 1)

            def tile0(t):
                score(t.ahead(AHEAD))
                mask(t)

            def factors(w, part):
                lo, hi = (0, FIRST[w]) if part == 0 else (FIRST[w], NBANKS[w])
                c = Chain(dve, own["coef"], 2 * w + part, 3)
                d, fac = by_bank(den, lo, hi), by_bank(coef, lo, hi)
                dens = den_of(BANK0[w], lo, hi)
                if part == 0:
                    dve.wait_ge(first_done, w + 1)
                    if w:
                        dve.wait_ge(freed_a, read_before(ACT_BANKS, w))
                else:
                    dve.wait_ge(tile_used, TILES * (w + 1))
                if w < L1:
                    f = by_bank(fe[:, w, :], lo, hi)
                    c.step(dve.tensor_tensor(d, dens, f, ALU.mult))
                    c.step(dve.tensor_scalar(d, d, TINY, None, ALU.max))
                    c.step(dve.reciprocal(d, d))
                    dve.tensor_tensor(fac, d, f, ALU.mult).then_inc(coef_done, 1)
                else:
                    empty = by_bank(none, lo, hi)
                    c.step(dve.tensor_scalar(empty, dens, 0.0, None, ALU.is_equal))
                    c.step(dve.tensor_tensor(d, dens, empty, ALU.add))
                    c.step(dve.reciprocal(fac, d))
                    dve.memset(scratch[:, 0:1], 0.0).then_inc(coef_done, 1)
                c.end()

            def read_out(w):
                def read(banks, part):
                    dve.wait_ge(coef_done, 2 * w + 1 + part)
                    for bank in banks:
                        for n in blocks_of(w, bank):
                            rows, factor = acc_of(n, BANK0[w])[:, 0:D], coef[:, n:n + 1]
                            if w < L1:
                                y = xs[:, w * HB + n, :]
                                ins = dve.scalar_tensor_tensor(out=y, in0=rows, scalar=factor, in1=y,
                                                               op0=ALU.mult, op1=ALU.add)
                            else:
                                ins = dve.tensor_scalar(obuf[:, obuf_row(w, n), :], rows, factor, 0.0,
                                                        ALU.mult, ALU.max)
                        ins.then_inc(freed_v, 1)

                early = 2 if w <= L1 else 1
                factors(w, 0)
                if w > L1:
                    dve.wait_ge(norm_done, GROUPS + (2 if w == L1 + 1 else 4))
                read(DVE_BANKS[w][:early], 0)
                factors(w, 1)
                read(DVE_BANKS[w][early:], 1)

            def moments(c, rows, k=0):
                dve.memset(scratch[:, 0:1], 0.0)
                for n in range(GROUP):
                    ins = dve.bn_stats(stats[:, n, :], rows(n))
                c.step(ins)
                dve.memset(scratch[:, 1:2], 0.0)
                for n in range(GROUP):
                    ins = dve.bn_aggr(mv[k][:, n, :], stats[:, n, :])
                c.step(ins)

            def variance(g):
                c = Chain(dve, own["var"], g, 2)
                if g:
                    dve.wait_ge(norm_done, g)
                if g % A_GROUPS == 0:
                    dve.wait_ge(freed_v, read_before(DVE_BANKS, g // A_GROUPS + 1))
                if g % A_GROUPS == SHARE // GROUP:
                    dve.wait_ge(y0_added, g // A_GROUPS + 1)
                moments(c, lambda n: xs[:, g * GROUP + n, :])
                dve.tensor_scalar(veps[0][:, :], mv[0][:, :, 1], EPS, None, ALU.add).then_inc(var_done, 1)
                c.end()

            def norm(g):
                dve.wait_ge(rstd_done, g + 1)
                dve.wait_ge(t_done, g)
                dve.wait_ge(x1_kept, g)
                for k in range(GROUP):
                    ins = dve.tensor_scalar(x1n[:, k, :], xs[:, g * GROUP + k, :], mv[0][:, k, 0:1],
                                            rstd[0][:, k:k + 1], ALU.subtract, ALU.mult)
                ins.then_inc(norm_done, 1)

            def powers(g):
                c = Chain(dve, own["pow"], g, 6)
                cols = slice(g * GROUP, (g + 1) * GROUP)
                dve.wait_ge(h_done, g + 1)
                c.step(dve.tensor_scalar(k_int[:, :], ps_t[:, 0:GROUP], LOG2E, None, ALU.mult))
                c.step(dve.scalar_tensor_tensor(out=u1[:, :], in0=k_int[:, :], scalar=-LN2_HI,
                                                in1=ps_t[:, 0:GROUP], op0=ALU.mult, op1=ALU.add))
                dve.scalar_tensor_tensor(out=u2[:, :], in0=k_int[:, :], scalar=-LN2_LO, in1=u1[:, :],
                                         op0=ALU.mult, op1=ALU.add).then_inc(u_done, 1)
                dve.tensor_copy(kf[:, cols], k_int[:, :])
                c.step(dve.tensor_reduce(hmax[:, :], ps_h[:, :].rearrange("p (k d) -> p k d", d=D),
                                         AX.X, ALU.max, apply_absolute_value=True))
                c.step(dve.tensor_scalar(hmax1[:, :], hmax[:, :], 1.0, None, ALU.max))
                c.step(dve.tensor_scalar(hexp[:, :], hmax1[:, :].bitcast(I32), EXP_MASK, None, ALU.bitwise_and))
                dve.tensor_scalar(hef[:, cols], hexp[:, :], 1.0 / EXPONENT, None, ALU.mult)
                c.step(dve.tensor_scalar(hinv[:, :], hexp[:, :], -1.0, float((254 + V_SCALE) * EXPONENT),
                                         ALU.mult, ALU.add))
                c.end()
                if g >= A_GROUPS:
                    mask_powers(1 + g - A_GROUPS, g * GROUP, GROUP)

            def parts(g):
                c = Chain(dve, own["parts"], g, 2)
                rows = V_v[:, g * GROUP:(g + 1) * GROUP, :]
                dve.wait_ge(r_done, g + 1)
                dve.tensor_tensor(q[:, :], rj[:, :], hinv[:, :].bitcast(F32), ALU.mult).then_inc(q_done, 1)
                dve.wait_ge(q_done, g + 1)
                c.step(dve.tensor_copy(rows[:, :, D], q[:, :]))
                c.step(dve.tensor_tensor(rows[:, :, DV + D], q[:, :], rows[:, :, D], ALU.subtract))
                c.end()

            def low(g):
                dve.wait_ge(hi_done, g + 1)
                for k in range(GROUP):
                    row = V_v[:, g * GROUP + k, :]
                    ins = dve.scalar_tensor_tensor(out=row[:, DV:DV + D], in0=ps_h[:, k * P:(k + 1) * P],
                                                   scalar=q[:, k:k + 1], in1=row[:, 0:D],
                                                   op0=ALU.mult, op1=ALU.subtract)
                ins.then_inc(v_done, 1)

            def mask_powers(call, t0, n):
                c = Chain(dve, own["mask"], call, 2)
                cols = slice(t0, t0 + n)
                c.step(dve.scalar_tensor_tensor(out=te[:, cols], in0=kf[:, cols], scalar=Kb[:, 0:1],
                                                in1=hef[:, cols], op0=ALU.subtract, op1=ALU.add))
                c.step(dve.tensor_scalar(tec[:, cols], te[:, cols], 254.0, 1.0, ALU.min, ALU.max))
                dve.tensor_scalar(pj[:, cols], tec[:, cols], float(EXPONENT), None, ALU.mult)\
                   .then_inc(p_done, 1)
                c.end()

            stages = {"variance": variance, "norm": norm, "powers": powers, "parts": parts, "low": low}

            copy_elr(0)
            dve.wait_ge(elr_copied, 1)
            for c in range(HALF // BANK):
                dve.wait_ge(el_copied, c + 1)
                cols = slice(c * BANK, (c + 1) * BANK)
                ins = dve.tensor_scalar(pair[:, 0, cols], elb[0][:, cols], elr[:, 0:1, 1], 0.0, ALU.add, ALU.max)
            ins.then_inc(scored_v, 1)
            score(Tile(0, 1))
            copy_elr(1)
            weigh_h(0)
            for jt in range(START):
                if jt == 1:
                    weigh_h(1)
                if 2 <= jt - 1 < H_GROUPS:
                    copy_elr(jt - 1)
                dve.wait_ge(elr_copied, min((jt + AHEAD) // 3 + 1, H_GROUPS))
                tile0(Tile(0, jt))
                if 2 <= jt - 1 < H_GROUPS:
                    weigh_h(jt - 1)
            dve.wait_ge(elr_copied, H_GROUPS)
            turns(dve, 0, START, TILES - RING, tile0, STEP)
            for jt in range(TILES - RING, TILES):
                if jt == TILES - AHEAD:
                    dve.wait_ge(el_copied, N // BANK)
                tile0(Tile(0, jt))
            dve.wait_ge(fe_done, 2)
            dve.wait_ge(xb_done, 1)
            for jt in range(TILES):
                if jt == 1:
                    read_out(0)
                for stage, g in plan0["dve"].get(jt, []):
                    stages[stage](g)
                if jt == 26:
                    dve.wait_ge(u_done, A_GROUPS)
                    dve.tensor_reduce(kpart[:, :], kf[:, 0:HB], AX.X, ALU.max).then_inc(k_part, 1)
                if jt == 30:
                    dve.wait_ge(k_row, 1)
                    dve.tensor_reduce(k1[:, :], ps_t[0:1, 0:P], AX.X, ALU.max).then_inc(k_one, 1)
                tile0(Tile(1, jt))
            c = Chain(dve, own["k"], 0, 1)
            dve.wait_ge(k_bcast, 1)
            c.step(dve.tensor_copy(Kb[:, :], ps_t[:, 256:257]))
            mask_powers(0, 0, HB)
            dve.wait_ge(p_done, 1)

            def scale(t):
                if t.resident:
                    return
                slot_free1(dve, t)
                s, cols = t.again_slot, BLOCKS[t.w] * P
                dve.wait_ge(again_in[s], 16 * (t.turn - L1 * TURNS + 1))
                dve.tensor_scalar(pair16[:, t.slot, 0:cols], adj_ring[:, s, 0:cols], 0.0,
                                  pj_f[:, bass.ds(t.jt, 1)], ALU.is_gt, ALU.mult).then_inc(scaled_v, 1)

            scale(Tile(L1, 1))
            scale(Tile(L1, 3))
            read_out(1)
            for jt in range(TILES):
                for stage, g in plan1["dve"].get(jt, []):
                    stages[stage](g)
                if jt >= RING:
                    if jt >= HB and jt % GROUP == 0:
                        dve.wait_ge(p_done, (jt - HB) // GROUP + 2)
                if jt == 26:
                    dve.wait_ge(t_copied, GROUPS)
                    dve.tensor_reduce(xtot[:, :], xsum[:, :], AX.X, ALU.add).then_inc(mean_in, 1)
                    dve.wait_ge(mean_in, 1)
                    dve.tensor_scalar(xmb[:, :], ones[:, :], xtot[:, 0:1], 1.0 / N, ALU.mult, ALU.mult)\
                       .then_inc(mean_in, 1)
                if jt >= RING:
                    scale(Tile(L1, jt))
            dve.wait_ge(x1_kept, GROUPS)
            dve.wait_ge(mean_mm, 1)
            dve.tensor_scalar(hmean[:, :], ps_t[:, 0:P], 0.0, None, ALU.max).then_inc(mean_done, 1)
            dve.wait_ge(mean_done, 1)
            c = Chain(dve, own["far"], 0, 3)
            dve.tensor_scalar(far[:, 0, :], te[:, :], TE_HIGH, None, ALU.is_gt)
            c.step(dve.tensor_scalar(far[:, 1, :], te[:, :], TE_LOW, None, ALU.is_lt))
            c.step(dve.tensor_reduce(far_any[:, :], far[:, :, :], AX.XY, ALU.add))
            dve.sem_inc(far_done, 1)

            def row_of(v, n):
                return v[:, bass.ds(n, 1), :].rearrange("p a d -> p (a d)")

            def last_y(g):
                rows, n0 = last_rows(g)
                if g < GROUPS - 2:
                    c = Chain(dve, own["stats"], g, 1)
                    dve.wait_ge(x1_added, g + 1)
                else:
                    c = Chain(dve, own["tail"], g - GROUPS + 2, 2)
                    c.step(dve.tensor_tensor(rows, rows, xs[:, g * GROUP:(g + 1) * GROUP, :], ALU.add))
                for n in range(GROUP):
                    ins = dve.scalar_tensor_tensor(out=rows[:, n, :], in0=hmean[:, :],
                                                   scalar=none[:, n0 + n:n0 + n + 1],
                                                   in1=rows[:, n, :], op0=ALU.mult, op1=ALU.add)
                c.step(ins)
                dve.memset(scratch[:, 0:1], 0.0)
                for n in range(GROUP):
                    ins = dve.bn_stats(stats[:, n, :], rows[:, n, :])
                ins.then_inc(stats_done, 1)
                c.end()

            def last_var(g):
                c = Chain(dve, own["mean"], g, 1)
                k = g % 2
                dve.wait_ge(stats_done, g + 1)
                if g >= 2:
                    dve.wait_ge(norm_done, GROUPS + g - 1)
                dve.memset(scratch[:, 1:2], 0.0)
                for n in range(GROUP):
                    ins = dve.bn_aggr(mv[k][:, n, :], stats[:, n, :])
                c.step(ins)
                dve.tensor_scalar(veps[k][:, :], mv[k][:, :, 1], EPS, None, ALU.add).then_inc(y_done, 1)
                c.end()

            def last_shift(g):
                k = g % 2
                dve.wait_ge(rstd_done, GROUPS + g + 1)
                dve.scalar_tensor_tensor(out=shift[k][:, :], in0=mv[k][:, :, 0], scalar=-1.0, in1=rstd[k][:, :],
                                         op0=ALU.mult, op1=ALU.mult).then_inc(shift_done, 1)

            stages = {"last_y": last_y, "last_var": last_var, "last_shift": last_shift}

            for w in (L1 + 1, L1 + 2):
                scale(Tile(w, 1))
                read_out(w - 1)
                scale(Tile(w, 3))
                for jt in range(RING, TILES):
                    for stage, k in plan2["dve"].get(jt, []):
                        stages[stage](k + (w - L1 - 1) * 3)
                    scale(Tile(w, jt))
                if w == L1 + 2:
                    dve.wait_ge(far_sum, 1)
                    dve.tensor_copy(flag[:, :], ps_t[0:1, 256:257]).then_inc(flag_done, 1)
            read_out(L1 + 2)
            dve.wait_ge(freed_v, read_before(DVE_BANKS, L1 + 3))
            dve.wait_ge(freed_a, read_before(ACT_BANKS, L1 + 3) - 1)
            last_y(GROUPS - 2)
            last_var(GROUPS - 2)
            dve.wait_ge(freed_a, read_before(ACT_BANKS, L1 + 3))
            last_y(GROUPS - 1)
            last_shift(GROUPS - 2)
            last_var(GROUPS - 1)
            g = GROUPS - 1
            dve.wait_ge(rstd_done, 2 * GROUPS)
            dve.wait_ge(stored[g % FIN], 16 * (g // FIN))
            for n in range(GROUP):
                ins = dve.tensor_scalar(fin[:, g % FIN * GROUP + n, :], last_rows(g)[0][:, n, :],
                                        mv[g % 2][:, n, 0:1], rstd[g % 2][:, n:n + 1], ALU.subtract, ALU.mult)
            ins.then_inc(last_done, 1)
            dve.wait_ge(flag_done, 1)
            for s in range(FIN):
                dve.wait_ge(stored[s], 16 * (GROUPS // FIN))
            dve.sem_inc(flag_done, 1)
            far_nodes = dve.value_load(flag[0:1, 0:1], min_val=0, max_val=N)
            with dve.If(far_nodes > 0):
                dve.tensor_scalar(wfb[:, :], ones[:, :], wf[:, 0:1], None, ALU.mult).then_inc(g_w, 1)
                dve.tensor_copy(x1n[:, :, :], xs[:, 0:GROUP, :]).then_inc(g_x, 1)
                with dve.Fori(0, GROUPS - 1) as g:
                    dve.wait_ge(g_hc, g + 1)
                    dve.tensor_copy(x1n[:, :, :], xs[:, bass.ds(g * GROUP + GROUP, GROUP), :]).then_inc(g_x, 1)
                dve.wait_ge(g_hc, GROUPS)
                dve.memset(scratch[:, :], 0.0).then_inc(g_e, 1)
                dve.wait_ge(g_e, 1)
                dve.memset(scratch[:, :], 0.0).then_inc(g_e, 1)
                dve.sem_inc(g_stored, 16)
                with dve.Fori(0, TILES) as t:
                    c = Chain(dve, g_own, t, 6)
                    dve.wait_ge(g_adj, t * 16 + 16)
                    dve.wait_ge(g_stored, t * 16 + 16)
                    dve.scalar_tensor_tensor(out=e_row, in0=adj_row, scalar=0.0, in1=fb, op0=ALU.is_gt, op1=ALU.mult)
                    c.step(dve.tensor_scalar(t_row, adj_row, 0.0, NEG_INF, ALU.is_le, ALU.mult))
                    dve.tensor_tensor(e_row, e_row, t_row, ALU.add).then_inc(g_e, 1)
                    dve.wait_ge(g_e, t * 3 + 3)
                    dve.tensor_reduce(g_max[:, :], e_row, AX.X, ALU.max, negate=True).then_inc(g_e, 1)
                    dve.wait_ge(g_e, t * 3 + 4)
                    dve.memset(scratch[:, 0:1], 0.0).then_inc(g_e, 1)
                    dve.wait_ge(g_exp, t + 1)
                    dve.wait_ge(g_acc, t + 1)
                    c.step(dve.reciprocal(g_rec[:, :], g_sum[:, :]))
                    c.step(dve.tensor_scalar(g_y[:, :], acc[:, 0, 0:D], g_rec[:, 0:1], 0.0, ALU.mult, ALU.max))
                    c.step(dve.tensor_tensor(g_y[:, :], g_y[:, :], row_of(xs, t), ALU.add))
                    dve.memset(scratch[:, 0:1], 0.0)
                    c.step(dve.bn_stats(stats[:, 0, :], g_y[:, :]))
                    dve.memset(scratch[:, 1:2], 0.0)
                    c.step(dve.bn_aggr(mv[0][:, 0, :], stats[:, 0, :]))
                    dve.tensor_scalar(veps[0][:, :], mv[0][:, :, 1], EPS, None, ALU.add).then_inc(g_var, 1)
                    dve.wait_ge(g_pow, t + 1)
                    dve.tensor_scalar(g_out[:, :], g_y[:, :], mv[0][:, 0, 0:1], rstd[0][:, 0:1],
                                      ALU.subtract, ALU.mult).then_inc(g_row, 1)
                    c.end()
                dve.wait_ge(g_stored, TILES * 16 + 16)

        @block.tensor
        def _(pe):
            pe.wait_ge(w_in, 16)
            pe.matmul(ps_t[:, 0:2], w0T, alr, start=True, stop=True)
            pe.matmul(ps_t[:, 8:9], waT, adst, start=True, stop=True).then_inc(wa_done, 1)
            pe.wait_ge(wa_copied, 2)
            pe.matmul(ps_t[:, 16:17], w1T_sb, wad[:, :], start=True, stop=True).then_inc(wa_done, 1)
            pe.wait_ge(wa_copied, 3)

            def el_rows(c):
                if c >= BANKS:
                    pe.wait_ge(el_copied, c - BANKS + 1)
                pe.matmul(el_bank(c), walb[:, :], xT_sb[:, c * BANK:(c + 1) * BANK],
                          start=True, stop=True).then_inc(el_done, 1)

            def h_tiles(a):
                if a >= 2:
                    pe.wait_ge(haug_done, a - 1)
                t0 = 3 * a
                for n in range(min(3, TILES - t0)):
                    if (t0 + n) % 8 == 0:
                        pe.wait_ge(xT_in[(t0 + n) // 8], 16)
                    ins = pe.matmul(small[a % 2][:, n * (D + 2):(n + 1) * (D + 2)],
                                    xT_sb[:, (t0 + n) * P:(t0 + n + 1) * P], w0, start=True, stop=True)
                ins.then_inc(h0_done, 1)

            pe.wait_ge(wa_copied, 4)
            pe.wait_ge(xT_in[0], 16)
            el_rows(0)
            el_rows(1)
            h_tiles(0)
            pe.wait_ge(xT_in[1], 16)
            el_rows(2)
            el_rows(3)
            h_tiles(1)
            for c in range(4, 8):
                if c % 2 == 0:
                    pe.wait_ge(xT_in[c // 2], 16)
                el_rows(c)

            def clear(bank):
                pe.matmul(acc[:, bank, 0:PER_BANK * DA], zeros[:, 0:P], zeros[:, :], start=True, stop=False,
                          skip_group_check=True)

            def bank_ready(w, bank):
                if w == 0:
                    pe.wait_ge(el_copied, N // BANK)
                else:
                    last = min(w, SWEEPS0 + 1) - 1
                    sem_, banks = (freed_v, DVE_BANKS) if bank in DVE_BANKS[last] else (freed_a, ACT_BANKS)
                    pe.wait_ge(sem_, read_before(banks, last, bank))

            def tile0(t):
                pe.wait_ge(masked, t.n + 1)
                for n in range(HB):
                    if t.first and n % PER_BANK == 0:
                        bank_ready(t.w, n // PER_BANK)
                        clear(n // PER_BANK)
                    ins = pe.matmul(acc_of(n), adj_ring[:, t.slot, n * P:(n + 1) * P],
                                    haug[:, bass.ds(t.jt, 1), :].rearrange("p a d -> p (a d)"),
                                    start=False, stop=t.last, skip_group_check=True)
                    if t.last and n == FIRST[t.w] * PER_BANK - 1:
                        ins.then_inc(first_done, 1)
                ins.then_inc(tile_used, 1)

            def turn(g):
                pe.wait_ge(norm_done, g + 1)
                if g:
                    pe.wait_ge(u_done, g)
                if g == A_GROUPS:
                    pe.wait_ge(p_done, 1)
                for k in range(GROUP):
                    ins = pe.transpose(ps_t[:, k * P:(k + 1) * P], x1n[:, k, :], ident)
                ins.then_inc(t_done, 1)

            def project(g):
                pe.wait_ge(t_copied, g + 1)
                if g:
                    pe.wait_ge(v_done, g)
                for k in range(GROUP):
                    pe.matmul(ps_h[:, k * P:(k + 1) * P], x1T[:, k * P:(k + 1) * P], w1_sb,
                              start=True, stop=True)
                for k in range(GROUP):
                    ins = pe.matmul(ps_t[:, k:k + 1], x1T[:, k * P:(k + 1) * P], wf[:, :], start=True, stop=True)
                ins.then_inc(h_done, 1)

            stages = {"turn": turn, "project": project}

            for jt in range(START):
                pe.wait_ge(haug_done, jt // 3 + 1)
                tile0(Tile(0, jt))
                if jt + 2 < H_GROUPS:
                    h_tiles(jt + 2)
            pe.wait_ge(haug_done, H_GROUPS)
            turns(pe, 0, START, TILES - RING, tile0, STEP)
            for jt in range(TILES - RING, TILES):
                tile0(Tile(0, jt))
            for jt in range(TILES):
                for stage, g in plan0["pe"].get(jt, []):
                    stages[stage](g)
                if jt == 28:
                    pe.wait_ge(k_part, 1)
                    pe.matmul(ps_t[0:1, 0:P], kpart[:, :], ident, start=True, stop=True).then_inc(k_row, 1)
                if jt == 30:
                    pe.wait_ge(k_one, 1)
                    pe.matmul(ps_t[:, 256:257], ones[0:1, 0:P], k1[:, :], start=True, stop=True)\
                      .then_inc(k_bcast, 1)
                tile0(Tile(1, jt))

            def tile1(t):
                pe.wait_ge(scaled_a if t.resident else scaled_v, (t.w - L1) * RESIDENT + t.half + 1)
                v = V_v[:, bass.ds(t.jt, 1), :].rearrange("p a c -> p (a c)")
                for n in range(BLOCKS[t.w]):
                    bank = BANK0[t.w] + n // PER_BANK
                    if t.first and n % PER_BANK == 0:
                        bank_ready(t.w, bank)
                        clear(bank)
                    for part in range(2):
                        ins = pe.matmul(acc_of(n, BANK0[t.w]), pair16[:, t.slot, n * P:(n + 1) * P],
                                        v[:, part * DV:part * DV + DA], start=False,
                                        stop=t.last, skip_group_check=True)
                    if t.last and n == FIRST[t.w] * PER_BANK - 1:
                        ins.then_inc(first_done, 1)
                ins.then_inc(tile_used, 1)

            for jt in range(TILES):
                for stage, g in plan1["pe"].get(jt, []):
                    stages[stage](g)
                if jt == 0 or jt >= HB and jt % GROUP == 0:
                    pe.wait_ge(v_done, max(jt // GROUP + 1, A_GROUPS))
                if jt == TILES - 2:
                    pe.wait_ge(mean_in, 2)
                    pe.matmul(ps_t[:, 0:P], xmb[:, :], w1_sb, start=True, stop=True).then_inc(mean_mm, 1)
                tile1(Tile(L1, jt))
            for w in (L1 + 1, L1 + 2):
                for jt in range(RING):
                    tile1(Tile(w, jt))
                if w == L1 + 2:
                    pe.wait_ge(far_done, 1)
                    pe.matmul(ps_t[0:1, 256:257], far_any[:, :], ones[:, 0:1], start=True, stop=True)\
                      .then_inc(far_sum, 1)
                turns(pe, w, RING, TILES - RING, tile1, STEP)
                for jt in range(TILES - RING, TILES):
                    tile1(Tile(w, jt))
            pe.wait_ge(flag_done, 2)
            far_nodes = pe.value_load(flag[0:1, 0:1], min_val=0, max_val=N)
            with pe.If(far_nodes > 0):
                pe.wait_ge(g_w, 1)
                with pe.Fori(0, GROUPS) as g:
                    pe.wait_ge(g_x, g + 1)
                    for k in range(GROUP):
                        ins = pe.transpose(ps_t[:, k * P:(k + 1) * P], x1n[:, k, :], ident)
                    ins.then_inc(g_t, 1)
                    pe.wait_ge(g_tc, g + 1)
                    pe.matmul(acc[:, 0, :], wfb[:, :], x1T[:, :], start=True, stop=True).then_inc(g_f, 1)
                    for k in range(GROUP):
                        ins = pe.matmul(acc[:, 1, k * P:(k + 1) * P], x1T[:, k * P:(k + 1) * P], w1_sb,
                                        start=True, stop=True)
                    ins.then_inc(g_h, 1)
                with pe.Fori(0, TILES) as t:
                    pe.wait_ge(g_exp, t + 1)
                    for c in range(GROUPS + 1):
                        if c < GROUPS:
                            if c >= 2:
                                pe.wait_ge(g_tcopy, t * GROUPS + c - 1)
                            for k in range(GROUP):
                                ins = pe.transpose(small[c % 2][:, k * P:(k + 1) * P],
                                                   e_row[:, (c * GROUP + k) * P:(c * GROUP + k + 1) * P], ident)
                            ins.then_inc(g_turn, 1)
                        if c:
                            pe.wait_ge(g_tcopy, t * GROUPS + c)
                            for k in range(GROUP):
                                jt = (c - 1) * GROUP + k
                                ins = pe.matmul(acc[:, 0, 0:D],
                                                t_row[:, (c - 1) % 2 * BANK + k * P:(c - 1) % 2 * BANK + (k + 1) * P],
                                                hfull[:, jt, :], start=jt == 0, stop=jt == TILES - 1)
                            if c == GROUPS:
                                ins.then_inc(g_acc, 1)


def kernel(x, adj, L0_gnn_weight, L0_gnn_a_l, L0_gnn_a_r, L0_gnn_b, L1_gnn_w, L1_gnn_w_a, L1_gnn_a):
    import concourse.bacc as bacc
    from concourse.bass_utils import run_bass_kernel_spmd

    x, adj = np.asarray(x), np.asarray(adj)
    W, w = np.asarray(L0_gnn_weight), np.asarray(L1_gnn_w)
    weights = np.zeros((P, W_COLS), np.float32)
    b = np.broadcast_to(np.asarray(L0_gnn_b), (P, D))
    a_lr = np.stack([np.asarray(L0_gnn_a_l), np.asarray(L0_gnn_a_r)], axis=1)
    parts = [W, W.T, w, w.T, b, np.eye(P, dtype=np.float32), a_lr,
             np.asarray(L1_gnn_w_a).T, np.asarray(L1_gnn_a)[2:4]]
    for part, at in zip(parts, W_AT):
        weights[:part.shape[0], at:at + part.shape[1]] = part
    arrays = {
        "adjT": adj.T.reshape(TILES, P, 2, HALF).transpose(2, 0, 1, 3),
        "adj": adj, "xT": x.T, "x": x, "weights": weights,
    }
    arrays = {"in_" + k: np.ascontiguousarray(v) for k, v in arrays.items()}
    nc = bacc.Bacc("TRN2", target_bir_lowering=False, num_devices=1)
    args = [nc.dram_tensor(k, v.shape, mybir.dt.from_np(v.dtype), kind="ExternalInput").ap()
            for k, v in arrays.items()]
    out = nc.dram_tensor("rows_out", (N, D), F32, kind="ExternalOutput").ap()
    build(nc, *args, out)
    r = run_bass_kernel_spmd(nc, [arrays], core_ids=[0])
    return r.results[0]["rows_out"]
```
